# Optimizing a Trainium2 kernel written in Bass

```python
import numpy as np
import jax
import jax.numpy as jnp

def _softmax(x, axis=-1):
    return jax.nn.softmax(x, axis=axis)

def _gelu(x):
    return jax.nn.gelu(x, approximate=True)

def _silu(x):
    return jax.nn.silu(x)

def _sigmoid(x):
    return jax.nn.sigmoid(x)

def _layernorm(x, axis=-1, eps=1e-05):
    m = jnp.mean(x, axis=axis, keepdims=True)
    v = jnp.var(x, axis=axis, keepdims=True)
    return (x - m) / jnp.sqrt(v + eps)

def _scatter_add(tgt, idx, src, axis=0):
    return tgt.at[idx].add(src)

def _segment_sum(src, seg, n):
    return jax.ops.segment_sum(src, seg, n)
kernel_name = 'mk_macaron_d1_jaxref_r8_429532'

def setup_inputs(seed: int=0):
    np.random.seed(seed)
    _w = jnp.asarray

    def _L0_attn_setup():
        import jax, jax.numpy as jnp
        import numpy as np
        B, S, D = (8, 256, 128)

        def _forward(x, W_qkv, b_qkv, W_vconv):
            b, s, d = x.shape
            qkv = x @ W_qkv + b_qkv
            q, k, v = jnp.split(qkv, 3, axis=-1)
            scores = jnp.einsum('bid,bjd->bij', q, k) * (1.0 / np.sqrt(d))
            mask = jnp.tril(jnp.ones((s, s), bool))
            scores = jnp.where(mask, scores, -jnp.inf)
            A = jax.nn.softmax(scores, axis=-1)
            w0, w1, w2 = (W_vconv[:, 0], W_vconv[:, 1], W_vconv[:, 2])
            v_prev = jnp.pad(v, ((0, 0), (1, 0), (0, 0)))[:, :s]
            v_next = jnp.pad(v, ((0, 0), (0, 1), (0, 0)))[:, 1:]
            C = w0 * v_prev + w1 * v + w2 * v_next
            out = jnp.einsum('bij,bjc->bic', A, C)
            diagA = jnp.diagonal(A, axis1=1, axis2=2)
            out = out - diagA[:, :, None] * (w2 * v_next)
            return out
        key = jax.random.key(seed)
        k0, k1, k2, k3 = jax.random.split(key, 4)
        x = jax.random.normal(k0, (B, S, D), jnp.float32)
        W_qkv = jax.random.normal(k1, (D, 3 * D), jnp.float32) * (1.0 / np.sqrt(D))
        b_qkv = jax.random.normal(k2, (3 * D,), jnp.float32) * 0.02
        W_vconv = jax.random.normal(k3, (D, 3), jnp.float32) * 0.02
        return {'x': x, 'W_qkv': W_qkv, 'b_qkv': b_qkv, 'W_vconv': W_vconv}
    _L0_attn_in = _L0_attn_setup()

    def _L0_ffn_setup():
        import jax, jax.numpy as jnp
        import numpy as np
        import math
        D_IN = 128
        FEATURES = (512, 512, 128)
        BATCH, SEQ = (8, 256)

        def _conn_dense(kernel_bool, x):
            w = jnp.where(kernel_bool, jnp.float32(1.0), jnp.float32(-1.0))
            return x @ w
        key = jax.random.key(seed)
        kx, kk0, kk1, kk2 = jax.random.split(key, 4)
        x = jax.random.normal(kx, (BATCH, SEQ, D_IN), dtype=jnp.float32)
        k0 = jax.random.randint(kk0, (2 * D_IN, FEATURES[0]), 0, 2).astype(jnp.bool_)
        k1 = jax.random.randint(kk1, (FEATURES[0], FEATURES[1]), 0, 2).astype(jnp.bool_)
        k2 = jax.random.randint(kk2, (FEATURES[1], FEATURES[2]), 0, 2).astype(jnp.bool_)
        s0 = jnp.asarray(1.0 / math.sqrt(2 * D_IN), dtype=jnp.float32)
        s1 = jnp.asarray(1.0 / math.sqrt(FEATURES[0]), dtype=jnp.float32)
        s2 = jnp.asarray(1.0 / math.sqrt(FEATURES[1]), dtype=jnp.float32)
        return {'x': x, 'k0': k0, 'k1': k1, 'k2': k2, 's0': s0, 's1': s1, 's2': s2}
    _L0_ffn_in = _L0_ffn_setup()
    _d = {'L0_attn_x': _L0_attn_in['x'], 'L0_attn_W_qkv': _L0_attn_in['W_qkv'], 'L0_attn_b_qkv': _L0_attn_in['b_qkv'], 'L0_attn_W_vconv': _L0_attn_in['W_vconv'], 'L0_ffn_k0': _L0_ffn_in['k0'], 'L0_ffn_k1': _L0_ffn_in['k1'], 'L0_ffn_k2': _L0_ffn_in['k2'], 'L0_ffn_s0': _L0_ffn_in['s0'], 'L0_ffn_s1': _L0_ffn_in['s1'], 'L0_ffn_s2': _L0_ffn_in['s2']}
    _x0 = _d['L0_attn_x']
    _d['L0_attn_x'] = jax.random.normal(jax.random.fold_in(jax.random.key(seed), 1), (8, 256, 128), dtype=_x0.dtype)
    del _x0
    return _d

def reference(L0_attn_x, L0_attn_W_qkv, L0_attn_b_qkv, L0_attn_W_vconv, L0_ffn_k0, L0_ffn_k1, L0_ffn_k2, L0_ffn_s0, L0_ffn_s1, L0_ffn_s2):

    def _L0_attn_ref(x, W_qkv, b_qkv, W_vconv):
        import jax, jax.numpy as jnp
        import numpy as np
        B, S, D = (8, 256, 128)

        def _forward(x, W_qkv, b_qkv, W_vconv):
            b, s, d = x.shape
            qkv = x @ W_qkv + b_qkv
            q, k, v = jnp.split(qkv, 3, axis=-1)
            scores = jnp.einsum('bid,bjd->bij', q, k) * (1.0 / np.sqrt(d))
            mask = jnp.tril(jnp.ones((s, s), bool))
            scores = jnp.where(mask, scores, -jnp.inf)
            A = jax.nn.softmax(scores, axis=-1)
            w0, w1, w2 = (W_vconv[:, 0], W_vconv[:, 1], W_vconv[:, 2])
            v_prev = jnp.pad(v, ((0, 0), (1, 0), (0, 0)))[:, :s]
            v_next = jnp.pad(v, ((0, 0), (0, 1), (0, 0)))[:, 1:]
            C = w0 * v_prev + w1 * v + w2 * v_next
            out = jnp.einsum('bij,bjc->bic', A, C)
            diagA = jnp.diagonal(A, axis1=1, axis2=2)
            out = out - diagA[:, :, None] * (w2 * v_next)
            return out
        return _forward(x, W_qkv, b_qkv, W_vconv)

    def _L0_ffn_ref(x, k0, k1, k2, s0, s1, s2):
        import jax, jax.numpy as jnp
        import numpy as np
        import math
        D_IN = 128
        FEATURES = (512, 512, 128)
        BATCH, SEQ = (8, 256)

        def _conn_dense(kernel_bool, x):
            w = jnp.where(kernel_bool, jnp.float32(1.0), jnp.float32(-1.0))
            return x @ w
        h = jnp.concatenate([x, -x], axis=-1)
        h = s0 * _conn_dense(k0, h)
        h = jax.nn.relu(h) * 2
        h = s1 * _conn_dense(k1, h)
        h = jax.nn.relu(h) * 2
        h = s2 * _conn_dense(k2, h)
        return h
    x = L0_attn_x
    x = x + 0.5 * _L0_ffn_ref(_layernorm(x, axis=-1), L0_ffn_k0, L0_ffn_k1, L0_ffn_k2, L0_ffn_s0, L0_ffn_s1, L0_ffn_s2)
    x = x + _L0_attn_ref(_layernorm(x, axis=-1), L0_attn_W_qkv, L0_attn_b_qkv, L0_attn_W_vconv)
    x = x + 0.5 * _L0_ffn_ref(_layernorm(x, axis=-1), L0_ffn_k0, L0_ffn_k1, L0_ffn_k2, L0_ffn_s0, L0_ffn_s1, L0_ffn_s2)
    return x

_drawn_inputs = setup_inputs


def setup_inputs(seed=0):
    import zlib

    import numpy as np

    out = dict(_drawn_inputs(seed))
    spreads = {}
    factors = {'L0_attn_W_qkv': 5.759, 'L0_attn_b_qkv': 8.0, 'L0_attn_W_vconv': 5.351}
    for name, (base, spread) in spreads.items():
        noise = np.random.default_rng([zlib.crc32(name.encode()), seed]).standard_normal(out[name].shape)
        drawn = base * np.exp(spread * noise) if base else spread * noise
        out[name] = jnp.asarray(drawn.astype(out[name].dtype))
    for name, factor in factors.items():
        out[name] = (out[name] * factor).astype(out[name].dtype)
    return out
```

```python
from contextlib import ExitStack

import concourse.bass as bass
from concourse import mybir

ALU = mybir.AluOpType
ACT = mybir.ActivationFunctionType
AX_X = mybir.AxisListType.X
F32 = mybir.dt.float32
F16 = mybir.dt.float16
BF16 = mybir.dt.bfloat16
U8 = mybir.dt.uint8

P = 128
LN_EPS = 1e-5
MASKED = -1e30

FFN1, FFN2, ATTN = 0, 1, 2

XN_SCALE = 2.0 ** 6
W1_SCALE = 2.0 ** -7


def macaron_kernel(nc, x, w_qkv, b_qkv, w_vconv, k0, k1, k2, s0, s1, s2, out):
    B, S, D = x.shape
    F = k1.shape[0]
    T = S // P
    FB = F // P
    HALF = FB // 2
    assert D == P and T == 2 and FB == 4 and k0.shape[0] == 2 * D and B > 4
    ATTN_SCALE = float(D) ** -0.5
    FINAL_SCALE = 0.5 * 2.0 * 2.0 * 2.0 / (XN_SCALE * W1_SCALE)

    with ExitStack() as ctx:
        def sb(name, shape, dt):
            return ctx.enter_context(nc.sbuf_tensor(name, shape, dt))

        def bank(name, count=1):
            return ctx.enter_context(nc.psum_tensor(name, [P, count, 512], F32))

        def sem(name):
            return ctx.enter_context(nc.semaphore(name))

        x_sb = sb("x_sb", [P, B, T, D], F32)
        k0_u8 = sb("k0_u8", [P, 2, F], U8)
        k1_u8 = sb("k1_u8", [P, FB, F], U8)
        k2_u8 = sb("k2_u8", [P, FB, D], U8)
        w0_diff = sb("w0_diff", [P, F], F16)
        w0 = sb("w0", [P, F], F16)
        w1 = sb("w1", [P, FB, F], F16)
        w2 = sb("w2", [P, FB, D], F16)
        wqkv = sb("wqkv", [P, 3, D], F32)
        bqkv = sb("bqkv", [P, 3], F32)
        wconv = sb("wconv", [P, 3], F32)
        neg_w2conv = sb("neg_w2conv", [P, 1], F32)
        s_cols = sb("s_cols", [P, 3], F32)
        s_pos = sb("s_pos", [P, 2], F32)
        s_neg = sb("s_neg", [P, 2], F32)
        s_sign = sb("s_sign", [P, 2], F32)
        s_abs = sb("s_abs", [P, 2], F32)
        w1_mul = sb("w1_mul", [P, 1], F32)
        w1_add = sb("w1_add", [P, 1], F32)
        ffn_fac_a = sb("ffn_fac_a", [P, 1], F32)
        ffn_fac = sb("ffn_fac", [P, 1], F32)
        zeros = sb("zeros", [P, P], F32)
        ident = sb("ident", [P, P], F32)
        ident_bf = sb("ident_bf", [P, P], BF16)
        mask_bf = sb("mask_bf", [P, P], BF16)
        neg_half = sb("neg_half", [P, T], F32)
        eps = sb("eps", [P, T], F32)

        ln_stats = [sb(f"ln_stats{k}", [P, T, 6], F32) for k in range(3)]
        ln_mv = [sb(f"ln_mv{k}", [P, T, 2], F32) for k in range(3)]
        ln_var = [sb(f"ln_var{k}", [P, T], F32) for k in range(3)]
        ln_rstd = [sb(f"ln_rstd{k}", [P, T], F32) for k in range(3)]
        xn = [sb(f"xn{k}", [P, T, D], F32) for k in range(3)]

        xt_hi = [sb(f"xt_hi{k}", [P, S], F16) for k in range(2)]
        xt_lo = [sb(f"xt_lo{k}", [P, S], F16) for k in range(2)]
        h1_hi = [sb(f"h1_hi{k}", [P, FB, S], F16) for k in range(2)]
        h1_lo = [sb(f"h1_lo{k}", [P, FB, S], F16) for k in range(2)]
        h2_hi = [sb(f"h2_hi{k}", [P, FB, S], F16) for k in range(2)]
        h2_lo = [sb(f"h2_lo{k}", [P, FB, S], F16) for k in range(2)]

        xt_attn = sb("xt_attn", [P, S], F32)
        q_t = sb("q_t", [P, S], F32)
        k_t = sb("k_t", [P, S], F32)
        v_t = sb("v_t", [P, S + 2], F32)
        next_t = sb("next_t", [P, S], F32)
        mid_t = sb("mid_t", [P, S], F32)
        prev_t = sb("prev_t", [P, S], F32)
        pm_t = sb("pm_t", [P, S], F32)
        conv_t = sb("conv_t", [P, S], F32)
        conv_next = sb("conv_next", [P, 2 * T, D], F32)
        neg_max = sb("neg_max", [P, T], F32)
        prob = sb("prob", [P, 3, P], F32)
        prob_sum = sb("prob_sum", [P, T], F32)
        prob_inv = sb("prob_inv", [P, T], F32)
        prob_t = sb("prob_t", [P, 3, P], F32)
        prob_diag = sb("prob_diag", [P, T, P], F32)

        ps_l1 = bank("ps_l1", 2)
        ps_l2 = bank("ps_l2", 2)
        ps_xt = bank("ps_xt")
        ps_l3 = bank("ps_l3")
        ps_a = bank("ps_a")
        ps_b = bank("ps_b")

        s_loaded = sem("s_loaded")
        k0_loaded, k1_loaded, k2_loaded = sem("k0_loaded"), sem("k1_loaded"), sem("k2_loaded")
        wqkv_loaded, attn_small_loaded = sem("wqkv_loaded"), sem("attn_small_loaded")
        X_PARTS = [(0, 1), (1, 2), (2, 4), (4, B)]
        x_loaded = [sem(f"x_loaded{i}") for i in range(len(X_PARTS))]
        stored = sem("stored")
        consts_step = sem("consts_step")
        consts_ready = sem("consts_ready")
        scal_step = sem("scal_step")
        scal_ready = sem("scal_ready")
        fac_ready = sem("fac_ready")
        w0_step, w0_ready, w1_ready, w2_ready = sem("w0_step"), sem("w0_ready"), sem("w1_ready"), sem("w2_ready")

        stats_done = [sem(f"stats_done{k}") for k in range(3)]
        mv_done = [sem(f"mv_done{k}") for k in range(3)]
        var_done = [sem(f"var_done{k}") for k in range(3)]
        rstd_done = [sem(f"rstd_done{k}") for k in range(3)]
        xn_ready = [sem(f"xn_ready{k}") for k in range(3)]
        xt_done = [sem(f"xt_done{k}") for k in range(3)]
        xt_hi_ready = [sem(f"xt_hi_ready{k}") for k in range(2)]
        xt_lo_ready = [sem(f"xt_lo_ready{k}") for k in range(2)]
        l1_done = [sem(f"l1_done{k}") for k in range(2)]
        h1_hi_ready = [sem(f"h1_hi_ready{k}") for k in range(2)]
        h1_lo_ready = [sem(f"h1_lo_ready{k}") for k in range(2)]
        l2_done = [sem(f"l2_done{k}") for k in range(2)]
        h2_hi_ready = [sem(f"h2_hi_ready{k}") for k in range(2)]
        h2_lo_ready = [sem(f"h2_lo_ready{k}") for k in range(2)]
        l3_done = [sem(f"l3_done{k}") for k in range(2)]
        res_done = [sem(f"res_done{k}") for k in range(3)]

        xt_attn_ready = sem("xt_attn_ready")
        q_done, kv_done = sem("q_done"), sem("kv_done")
        q_ready, k_ready, v_ready = sem("q_ready"), sem("k_ready"), sem("v_ready")
        taps_done = sem("taps_done")
        pm_done = sem("pm_done")
        conv_ready = sem("conv_ready")
        scores_done = sem("scores_done")
        max_ready = sem("max_ready")
        probs_ready = sem("probs_ready")
        diag_ready = sem("diag_ready")
        inv_ready = sem("inv_ready")
        conv_next_done, conv_next_ready = sem("conv_next_done"), sem("conv_next_ready")
        prob_t_done, prob_t_ready = sem("prob_t_done"), sem("prob_t_ready")
        attn_out_done = sem("attn_out_done")

        ATTN_LAG, FFN2_LAG, L3_LAG = 1, 2, 3
        ITERS = B + L3_LAG
        LOOP_FROM, LOOP_TO = L3_LAG, B - 1

        def iterations(engine, body):
            for t in range(LOOP_FROM):
                body(t, lambda b: 0 <= b < B)
            with engine.Fori(LOOP_FROM, LOOP_TO) as t:
                body(t, lambda b: True)
            for t in range(LOOP_TO, ITERS):
                body(t, lambda b: 0 <= b < B)

        block = ctx.enter_context(nc.Block())

        @block.sync
        def _(sp):
            def load_x(part):
                a, z = X_PARTS[part]
                sp.dma_start(x_sb[:, a:z], x[a:z].rearrange("b (t p) d -> p b t d", p=P)).then_inc(x_loaded[part], 16)

            load_x(0)
            sp.dma_start(k0_u8[:], k0.rearrange("(c p) f -> p c f", p=P)).then_inc(k0_loaded, 16)
            sp.dma_start(wqkv[:], w_qkv.rearrange("p (c d) -> p c d", c=3)).then_inc(wqkv_loaded, 16)
            for part in range(1, len(X_PARTS)):
                load_x(part)
            with sp.Fori(0, B) as b:
                sp.wait_ge(res_done[FFN2], b + 1)
                sp.dma_start(out[b].rearrange("(t p) d -> p t d", p=P), x_sb[:, b]).then_inc(stored, 16)
            sp.wait_ge(stored, 16 * B)

        @block.gpsimd
        def _(pool):
            pool.dma_start(bqkv[:], b_qkv).then_inc(attn_small_loaded, 16)
            pool.dma_start(wconv[:], w_vconv).then_inc(attn_small_loaded, 16)
            nc.gpsimd.memset(zeros[:], 0.0).then_inc(consts_step, 1)
            nc.gpsimd.memset(neg_half[:], -0.5).then_inc(consts_step, 1)
            nc.gpsimd.memset(v_t[:, 0:1], 0.0).then_inc(consts_step, 1)
            nc.gpsimd.memset(v_t[:, S + 1:S + 2], 0.0).then_inc(consts_step, 1)
            nc.gpsimd.memset(eps[:], LN_EPS).then_inc(consts_step, 1)
            pool.wait_ge(consts_step, 5)
            nc.gpsimd.affine_select(out=ident[:], in_=zeros[:], compare_op=ALU.not_equal, fill=1.0, base=0,
                                    pattern=[[-1, P]], channel_multiplier=1).then_inc(consts_ready, 1)
            nc.gpsimd.affine_select(out=ident_bf[:], in_=zeros[:], compare_op=ALU.not_equal, fill=1.0, base=0,
                                    pattern=[[-1, P]], channel_multiplier=1).then_inc(consts_ready, 1)
            nc.gpsimd.affine_select(out=mask_bf[:], in_=zeros[:], compare_op=ALU.is_ge, fill=MASKED, base=0,
                                    pattern=[[-1, P]], channel_multiplier=1).then_inc(consts_ready, 1)

            def rstd(k, b):
                pool.wait_ge(mv_done[k], T * (b + 1))
                nc.gpsimd.tensor_tensor(ln_var[k][:], ln_mv[k][:, :, 1], eps[:], ALU.add).then_inc(var_done[k], 1)
                pool.wait_ge(var_done[k], b + 1)
                nc.gpsimd.tensor_tensor(ln_rstd[k][:], ln_var[k][:], neg_half[:], ALU.pow).then_inc(rstd_done[k], 1)

            def conv_values(b):
                pool.wait_ge(v_ready, b + 1)
                for tap, (dst, w) in enumerate(((prev_t, wconv[:, 0:1]), (mid_t, wconv[:, 1:2]), (next_t, neg_w2conv[:]))):
                    nc.gpsimd.tensor_tensor(dst[:], v_t[:, tap:tap + S], w.to_broadcast([P, S]), ALU.mult).then_inc(taps_done, 1)
                pool.wait_ge(taps_done, 3 * (b + 1))
                nc.gpsimd.tensor_tensor(pm_t[:], prev_t[:], mid_t[:], ALU.add).then_inc(pm_done, 1)
                pool.wait_ge(pm_done, b + 1)
                nc.gpsimd.tensor_tensor(conv_t[:], pm_t[:], next_t[:], ALU.subtract).then_inc(conv_ready, 1)

            def diagonal(b):
                pool.wait_ge(probs_ready, T * (b + 1))
                for i in range(T):
                    last = nc.gpsimd.tensor_tensor(prob_diag[:, i], prob[:, 2 * i], ident[:], ALU.mult)
                last.then_inc(diag_ready, 1)

            def body(t, live):
                if live(t - ATTN_LAG):
                    conv_values(t - ATTN_LAG)
                if live(t + 1):
                    rstd(FFN1, t + 1)
                if live(t - ATTN_LAG):
                    diagonal(t - ATTN_LAG)
                if live(t):
                    rstd(ATTN, t)
                if live(t - ATTN_LAG):
                    rstd(FFN2, t - ATTN_LAG)

            pool.wait_ge(attn_small_loaded, 32)
            nc.gpsimd.tensor_scalar(neg_w2conv[:], wconv[:, 2:3], -1.0, 1.0, ALU.mult, ALU.mult).then_inc(consts_step, 1)
            pool.wait_ge(consts_step, 6)
            rstd(FFN1, 0)
            iterations(pool, body)

        @block.scalar
        def _(act):
            for i, s in enumerate((s0, s1, s2)):
                act.dma_start(s_cols[:, i:i + 1], s.partition_broadcast(P)).then_inc(s_loaded, 16)
            act.dma_start(k1_u8[:], k1.rearrange("(c p) f -> p c f", p=P)).then_inc(k1_loaded, 16)
            act.dma_start(k2_u8[:], k2.rearrange("(c p) f -> p c f", p=P)).then_inc(k2_loaded, 16)

            def split_hi_xt(k, b):
                act.wait_ge(xt_done[k], b + 1)
                nc.scalar.activation(xt_hi[k][:], ps_xt[:, 0, 0:S], ACT.Copy, scale=XN_SCALE).then_inc(xt_hi_ready[k], 1)

            def split_hi(k, b, half, done, ps, hi, ready):
                act.wait_ge(done[k], 2 * b + half + 1)
                nc.scalar.activation(hi[k][:, HALF * half:HALF * half + HALF], ps[:, half], ACT.Relu).then_inc(ready[k], 1)

            def h1_hi_half(k, b, half):
                split_hi(k, b, half, l1_done, ps_l1, h1_hi, h1_hi_ready)

            def h2_hi_half(k, b, half):
                split_hi(k, b, half, l2_done, ps_l2, h2_hi, h2_hi_ready)

            def copy_xt_attn(b):
                act.wait_ge(xt_done[ATTN], b + 1)
                nc.scalar.copy(xt_attn[:], ps_a[:, 0, 0:S]).then_inc(xt_attn_ready, 1)

            def kv_bias(b):
                act.wait_ge(kv_done, b + 1)
                nc.scalar.activation(k_t[:], ps_b[:, 0, 0:S], ACT.Identity, bias=bqkv[:, 1:2]).then_inc(k_ready, 1)
                if not isinstance(b, int) or b > 0:
                    act.wait_ge(conv_ready, b)
                nc.scalar.activation(v_t[:, 1:S + 1], ps_b[:, 0, S:2 * S], ACT.Identity, bias=bqkv[:, 2:3]).then_inc(v_ready, 1)

            def softmax_exp(b):
                act.wait_ge(max_ready, T * (b + 1))
                nc.scalar.activation(prob[:, 0], ps_b[:, 0, 0:P], ACT.Exp, bias=neg_max[:, 0:1],
                                     accum_out=prob_sum[:, 0:1]).then_inc(probs_ready, 1)
                nc.scalar.activation(prob[:, 1:3], ps_b[:, 0, P:3 * P], ACT.Exp, bias=neg_max[:, 1:2],
                                     accum_out=prob_sum[:, 1:2]).then_inc(probs_ready, 1)

            def copy_conv_next(b):
                act.wait_ge(conv_next_done, b + 1)
                nc.scalar.copy(conv_next[:], ps_a[:, 0]).then_inc(conv_next_ready, 1)

            def copy_prob_t(b):
                act.wait_ge(prob_t_done, b + 1)
                nc.scalar.copy(prob_t[:], ps_b[:, 0, 0:3 * P]).then_inc(prob_t_ready, 1)

            def body(t, live):
                a, f = t - ATTN_LAG, t - FFN2_LAG
                if live(t):
                    split_hi_xt(FFN1, t)
                if live(a):
                    copy_xt_attn(a)
                if live(t):
                    h1_hi_half(FFN1, t, 0)
                    h1_hi_half(FFN1, t, 1)
                if live(a):
                    kv_bias(a)
                if live(t):
                    h2_hi_half(FFN1, t, 0)
                if live(f):
                    split_hi_xt(FFN2, f)
                if live(a):
                    softmax_exp(a)
                if live(t):
                    h2_hi_half(FFN1, t, 1)
                if live(f):
                    h1_hi_half(FFN2, f, 0)
                    h1_hi_half(FFN2, f, 1)
                if live(a):
                    copy_conv_next(a)
                    copy_prob_t(a)
                if live(f):
                    h2_hi_half(FFN2, f, 0)
                    h2_hi_half(FFN2, f, 1)

            act.wait_ge(scal_ready, 1)
            act.wait_ge(k1_loaded, 16)
            nc.scalar.activation(w1[:], k1_u8[:], ACT.Identity, bias=w1_add[:], scale=w1_mul[:]).then_inc(w1_ready, 1)
            act.wait_ge(attn_small_loaded, 32)
            act.wait_ge(consts_step, 5)
            iterations(act, body)

        @block.vector
        def _(dve):
            def source_ready(k, b):
                if k == FFN1:
                    part = next(i for i, (a, z) in enumerate(X_PARTS) if b < z) if isinstance(b, int) else len(X_PARTS) - 1
                    dve.wait_ge(x_loaded[part], 16)
                else:
                    wait_apart(res_done[FFN1 if k == ATTN else ATTN], (b + 1) * (1 if k == ATTN else T))

            def wait_apart(semaphore, value):
                if not isinstance(value, int):
                    register = dve.to_reg(value)
                dve.wait_ge(s_loaded, 48)
                dve.wait_ge(semaphore, value)

            def ln_moments(k, b):
                source_ready(k, b)
                for i in range(T):
                    nc.vector.bn_stats(ln_stats[k][:, i], x_sb[:, b, i]).then_inc(stats_done[k], 1)
                wait_apart(stats_done[k], T * (b + 1))
                for i in range(T):
                    nc.vector.bn_aggr(ln_mv[k][:, i], ln_stats[k][:, i]).then_inc(mv_done[k], 1)

            def ln_apply(k, b):
                dve.wait_ge(rstd_done[k], b + 1)
                if not isinstance(b, int) or b > 0:
                    dve.wait_ge(xt_done[k], b)
                for i in range(T):
                    last = nc.vector.tensor_scalar(xn[k][:, i], x_sb[:, b, i], ln_mv[k][:, i, 0:1],
                                                   ln_rstd[k][:, i:i + 1], ALU.subtract, ALU.mult)
                last.then_inc(xn_ready[k], 1)

            def split_lo_xt(k, b):
                dve.wait_ge(xt_hi_ready[k], b + 1)
                nc.vector.scalar_tensor_tensor(out=xt_lo[k][:], in0=ps_xt[:, 0, 0:S], scalar=XN_SCALE, in1=xt_hi[k][:],
                                               op0=ALU.mult, op1=ALU.subtract).then_inc(xt_lo_ready[k], 1)

            def split_lo(k, b, half, ps, hi, lo, hi_ready, lo_ready):
                dve.wait_ge(hi_ready[k], 2 * b + half + 1)
                blocks = slice(HALF * half, HALF * half + HALF)
                nc.vector.scalar_tensor_tensor(out=lo[k][:, blocks], in0=ps[:, half], scalar=0.0, in1=hi[k][:, blocks],
                                               op0=ALU.max, op1=ALU.subtract).then_inc(lo_ready[k], 1)

            def h1_lo_half(k, b, half):
                split_lo(k, b, half, ps_l1, h1_hi, h1_lo, h1_hi_ready, h1_lo_ready)

            def h2_lo_half(k, b, half):
                split_lo(k, b, half, ps_l2, h2_hi, h2_lo, h2_hi_ready, h2_lo_ready)

            def ffn_residual(k, b):
                dve.wait_ge(l3_done[k], b + 1)
                nc.vector.scalar_tensor_tensor(out=x_sb[:, b], in0=ps_l3[:, 0, 0:T * D], scalar=ffn_fac[:], in1=x_sb[:, b],
                                               op0=ALU.mult, op1=ALU.add).then_inc(res_done[k], 1)

            def q_bias_scale(b):
                dve.wait_ge(q_done, b + 1)
                nc.vector.tensor_scalar(q_t[:], ps_a[:, 0, 0:S], bqkv[:, 0:1], ATTN_SCALE, ALU.add, ALU.mult).then_inc(q_ready, 1)

            def softmax_max(b):
                dve.wait_ge(scores_done, b + 1)
                for i, (a, z) in enumerate(((0, P), (P, 3 * P))):
                    nc.vector.tensor_reduce(neg_max[:, i:i + 1], ps_b[:, 0, a:z], AX_X, ALU.max, negate=True).then_inc(max_ready, 1)

            def softmax_inverse(b):
                dve.wait_ge(probs_ready, T * (b + 1))
                nc.vector.reciprocal(prob_inv[:], prob_sum[:]).then_inc(inv_ready, 1)

            def attn_residual(b):
                dve.wait_ge(inv_ready, b + 1)
                dve.wait_ge(attn_out_done, b + 1)
                for i in range(T):
                    nc.vector.scalar_tensor_tensor(out=x_sb[:, b, i], in0=ps_a[:, 0, i * D:(i + 1) * D], scalar=prob_inv[:, i:i + 1],
                                                   in1=x_sb[:, b, i], op0=ALU.mult, op1=ALU.add).then_inc(res_done[ATTN], 1)

            def body(t, live):
                a, f, g = t - ATTN_LAG, t - FFN2_LAG, t - L3_LAG
                if live(t):
                    split_lo_xt(FFN1, t)
                    h1_lo_half(FFN1, t, 0)
                    h1_lo_half(FFN1, t, 1)
                if live(f):
                    ln_apply(FFN2, f)
                if live(a):
                    q_bias_scale(a)
                if live(g):
                    ffn_residual(FFN2, g)
                if live(t):
                    h2_lo_half(FFN1, t, 0)
                if live(f):
                    split_lo_xt(FFN2, f)
                if live(a):
                    softmax_max(a)
                if live(t):
                    h2_lo_half(FFN1, t, 1)
                if live(f):
                    h1_lo_half(FFN2, f, 0)
                    h1_lo_half(FFN2, f, 1)
                if live(t + 1):
                    ln_moments(FFN1, t + 1)
                if live(a):
                    softmax_inverse(a)
                if live(t + 1):
                    ln_apply(FFN1, t + 1)
                if live(t):
                    ffn_residual(FFN1, t)
                    ln_moments(ATTN, t)
                if live(a):
                    attn_residual(a)
                    ln_moments(FFN2, a)
                if live(t):
                    ln_apply(ATTN, t)
                if live(f):
                    h2_lo_half(FFN2, f, 0)
                    h2_lo_half(FFN2, f, 1)

            dve.wait_ge(s_loaded, 48)
            nc.vector.tensor_scalar(s_pos[:], s_cols[:, 0:2], 0.0, None, ALU.is_gt).then_inc(scal_step, 1)
            nc.vector.tensor_scalar(s_neg[:], s_cols[:, 0:2], 0.0, None, ALU.is_lt).then_inc(scal_step, 1)
            dve.wait_ge(scal_step, 2)
            nc.vector.tensor_tensor(s_sign[:], s_pos[:], s_neg[:], ALU.subtract).then_inc(scal_step, 1)
            dve.wait_ge(scal_step, 3)
            nc.vector.tensor_scalar(w1_mul[:], s_sign[:, 1:2], 2.0 * W1_SCALE, None, ALU.mult)
            nc.vector.tensor_scalar(w1_add[:], s_sign[:, 1:2], -W1_SCALE, None, ALU.mult).then_inc(scal_ready, 1)
            ln_moments(FFN1, 0)
            dve.wait_ge(k0_loaded, 16)
            nc.vector.tensor_tensor(w0_diff[:], k0_u8[:, 0], k0_u8[:, 1], ALU.subtract).then_inc(w0_step, 1)
            dve.wait_ge(w0_step, 1)
            nc.vector.tensor_scalar(w0[:], w0_diff[:], s_sign[:, 0:1], None, ALU.mult).then_inc(w0_ready, 1)
            ln_apply(FFN1, 0)
            nc.vector.tensor_tensor(s_abs[:], s_cols[:, 0:2], s_sign[:], ALU.mult).then_inc(scal_step, 1)
            dve.wait_ge(scal_step, 4)
            nc.vector.tensor_tensor(ffn_fac_a[:], s_abs[:, 0:1], s_abs[:, 1:2], ALU.mult).then_inc(scal_step, 1)
            dve.wait_ge(scal_step, 5)
            nc.vector.scalar_tensor_tensor(out=ffn_fac[:], in0=ffn_fac_a[:], scalar=FINAL_SCALE, in1=s_cols[:, 2:3],
                                           op0=ALU.mult, op1=ALU.mult).then_inc(fac_ready, 1)
            dve.wait_ge(k2_loaded, 16)
            nc.vector.tensor_scalar(w2[:], k2_u8[:], 2.0, -1.0, ALU.mult, ALU.add).then_inc(w2_ready, 1)
            dve.wait_ge(attn_small_loaded, 32)
            dve.wait_ge(fac_ready, 1)
            iterations(dve, body)

        @block.tensor
        def _(pe):
            def transpose_rows(k, b):
                pe.wait_ge(xn_ready[k], b + 1)
                ps = ps_a if k == ATTN else ps_xt
                if k == ATTN and (not isinstance(b, int) or b > 0):
                    pe.wait_ge(res_done[ATTN], T * b)
                for i in range(T):
                    last = nc.tensor.transpose(ps[:, 0, i * P:(i + 1) * P], xn[k][:, i], ident[:])
                last.then_inc(xt_done[k], 1)

            def layer1(k, b):
                pe.wait_ge(xt_lo_ready[k], b + 1)
                for half in range(2):
                    for c in range(HALF):
                        block_out = HALF * half + c
                        w = w0[:, block_out * P:(block_out + 1) * P]
                        dst = ps_l1[:, half, c * S:(c + 1) * S]
                        nc.tensor.matmul(dst, w, xt_hi[k][:], start=True, stop=False)
                        last = nc.tensor.matmul(dst, w, xt_lo[k][:], start=False, stop=True)
                    last.then_inc(l1_done[k], 1)

            def layer2_half(k, b, half):
                for c in range(HALF):
                    block_out = HALF * half + c
                    dst = ps_l2[:, half, c * S:(c + 1) * S]
                    for j in range(FB):
                        if half == 0 and c == 0 and j % HALF == 0:
                            pe.wait_ge(h1_lo_ready[k], 2 * b + j // HALF + 1)
                        w = w1[:, j, block_out * P:(block_out + 1) * P]
                        nc.tensor.matmul(dst, w, h1_hi[k][:, j], start=(j == 0), stop=False)
                        last = nc.tensor.matmul(dst, w, h1_lo[k][:, j], start=False, stop=(j == FB - 1))
                last.then_inc(l2_done[k], 1)

            def layer3(k, b):
                if k == FFN1 and (not isinstance(b, int) or b >= L3_LAG):
                    pe.wait_ge(res_done[FFN2], b - L3_LAG + 1)
                if k == FFN1 and isinstance(b, int) and 0 < b < L3_LAG:
                    pe.wait_ge(res_done[FFN1], b)
                if k == FFN2:
                    if isinstance(b, int):
                        pe.wait_ge(res_done[FFN1], min(b + L3_LAG, B))
                        if b + L3_LAG > B:
                            pe.wait_ge(res_done[FFN2], b)
                    else:
                        pe.wait_ge(res_done[FFN1], b + L3_LAG)
                pe.wait_ge(h2_lo_ready[k], 2 * (b + 1))
                for i in range(T):
                    for j in range(FB):
                        rows = slice(i * P, (i + 1) * P)
                        dst = ps_l3[:, 0, i * D:(i + 1) * D]
                        nc.tensor.matmul(dst, h2_hi[k][:, j, rows], w2[:, j], start=(j == 0), stop=False)
                        last = nc.tensor.matmul(dst, h2_lo[k][:, j, rows], w2[:, j], start=False, stop=(j == FB - 1))
                last.then_inc(l3_done[k], 1)

            def project_qkv(b):
                pe.wait_ge(xt_attn_ready, b + 1)
                nc.tensor.matmul(ps_b[:, 0, 0:S], wqkv[:, 1], xt_attn[:], start=True, stop=True)
                nc.tensor.matmul(ps_b[:, 0, S:2 * S], wqkv[:, 2], xt_attn[:], start=True, stop=True).then_inc(kv_done, 1)
                nc.tensor.matmul(ps_a[:, 0, 0:S], wqkv[:, 0], xt_attn[:], start=True, stop=True).then_inc(q_done, 1)

            def scores(b):
                pe.wait_ge(q_ready, b + 1)
                pe.wait_ge(k_ready, b + 1)
                pe.wait_ge(v_ready, b + 1)
                nc.tensor.matmul(ps_b[:, 0, 0:P], q_t[:, 0:P], k_t[:, 0:P], start=True, stop=False)
                nc.tensor.matmul(ps_b[:, 0, 0:P], ident_bf[:], mask_bf[:], start=False, stop=True)
                nc.tensor.matmul(ps_b[:, 0, P:3 * P], q_t[:, P:S], k_t[:], start=True, stop=False, skip_group_check=True)
                nc.tensor.matmul(ps_b[:, 0, 2 * P:3 * P], ident_bf[:], mask_bf[:], start=False, stop=True,
                                 skip_group_check=True).then_inc(scores_done, 1)

            def transpose_conv(b):
                pe.wait_ge(conv_ready, b + 1)
                for n, src in enumerate((conv_t, next_t)):
                    for i in range(T):
                        last = nc.tensor.transpose(ps_a[:, 0, (T * n + i) * P:(T * n + i + 1) * P], src[:, i * P:(i + 1) * P], ident[:])
                last.then_inc(conv_next_done, 1)

            def transpose_probs(b):
                pe.wait_ge(probs_ready, T * (b + 1))
                for n in range(3):
                    last = nc.tensor.transpose(ps_b[:, 0, n * P:(n + 1) * P], prob[:, n], ident[:])
                last.then_inc(prob_t_done, 1)

            def attend(b):
                pe.wait_ge(conv_next_ready, b + 1)
                pe.wait_ge(prob_t_ready, b + 1)
                pe.wait_ge(diag_ready, b + 1)
                for i in range(T):
                    dst = ps_a[:, 0, i * D:(i + 1) * D]
                    for j in range(i + 1):
                        nc.tensor.matmul(dst, prob_t[:, i + j], conv_next[:, j], start=(j == 0), stop=False)
                    last = nc.tensor.matmul(dst, prob_diag[:, i], conv_next[:, T + i], start=False, stop=True)
                last.then_inc(attn_out_done, 1)

            def body(t, live):
                a, f, g = t - ATTN_LAG, t - FFN2_LAG, t - L3_LAG
                if live(t):
                    transpose_rows(FFN1, t)
                if live(a):
                    transpose_rows(ATTN, a)
                if live(t):
                    layer1(FFN1, t)
                if live(a):
                    project_qkv(a)
                if live(g):
                    layer3(FFN2, g)
                if live(t):
                    layer2_half(FFN1, t, 0)
                if live(f):
                    transpose_rows(FFN2, f)
                if live(a):
                    scores(a)
                if live(t):
                    layer2_half(FFN1, t, 1)
                if live(f):
                    layer1(FFN2, f)
                if live(a):
                    transpose_conv(a)
                    transpose_probs(a)
                if live(t):
                    layer3(FFN1, t)
                if live(a):
                    attend(a)
                if live(f):
                    layer2_half(FFN2, f, 0)
                    layer2_half(FFN2, f, 1)

            pe.wait_ge(consts_ready, 3)
            pe.wait_ge(w0_ready, 1)
            pe.wait_ge(w1_ready, 1)
            pe.wait_ge(w2_ready, 1)
            pe.wait_ge(wqkv_loaded, 16)
            iterations(pe, body)


_INS = ['L0_attn_x', 'L0_attn_W_qkv', 'L0_attn_b_qkv', 'L0_attn_W_vconv', 'L0_ffn_k0', 'L0_ffn_k1', 'L0_ffn_k2',
        'L0_ffn_s0', 'L0_ffn_s1', 'L0_ffn_s2']


def kernel(**inputs):
    import numpy as np
    import concourse.bacc as bacc
    from concourse.bass_utils import run_bass_kernel_spmd

    nc = bacc.Bacc("TRN2", target_bir_lowering=False, num_devices=1)
    arrays, args = {}, []
    for name in _INS:
        a = np.ascontiguousarray(inputs[name])
        if a.ndim == 0 or name[-2:] in ("s0", "s1", "s2"):
            a = a.reshape(1, 1)
        if name.endswith("b_qkv"):
            a = np.ascontiguousarray(a.reshape(3, -1).T)
        arrays[f"in_{name}"] = a
        args.append(nc.dram_tensor(f"in_{name}", a.shape, mybir.dt.from_np(a.dtype), kind="ExternalInput").ap())
    x_shape = inputs['L0_attn_x'].shape
    out = nc.dram_tensor("out_y", x_shape, F32, kind="ExternalOutput").ap()
    macaron_kernel(nc, *args, out)
    r = run_bass_kernel_spmd(nc, [arrays], core_ids=[0])
    return r.results[0]["out_y"]
```

```python
from contextlib import ExitStack

import concourse.bass as bass
from concourse import mybir

ALU = mybir.AluOpType
ACT = mybir.ActivationFunctionType
AX_X = mybir.AxisListType.X
F32 = mybir.dt.float32
F16 = mybir.dt.float16
BF16 = mybir.dt.bfloat16
U8 = mybir.dt.uint8

P = 128
LN_EPS = 1e-5
MASKED = -1e30
WARM_UP = 10

SLOTS, ATTN = 4, 2

XN_SCALE = 2.0 ** 6
W1_SCALE = 2.0 ** -7


def macaron_kernel(nc, x, w_qkv, attn_cols, k0, k1, k2, scalars, out):
    B, S, D = x.shape
    F = k1.shape[0]
    T = S // P
    FB = F // P
    HALF = FB // 2
    assert D == P and T == 2 and FB == 4 and k0.shape[0] == 2 * D and B == 8
    ATTN_SCALE = float(D) ** -0.5
    FINAL_SCALE = 0.5 * 2.0 * 2.0 * 2.0 / (XN_SCALE * W1_SCALE)

    with ExitStack() as ctx:
        def sb(name, shape, dt):
            return ctx.enter_context(nc.sbuf_tensor(name, shape, dt))

        def bank(name, count=1):
            return ctx.enter_context(nc.psum_tensor(name, [P, count, 512], F32))

        def sem(name):
            return ctx.enter_context(nc.semaphore(name))

        x_sb = sb("x_sb", [P, B, T, D], F32)
        k0_u8 = sb("k0_u8", [P, 2, F], U8)
        k1_u8 = sb("k1_u8", [P, FB, F], U8)
        k2_u8 = sb("k2_u8", [P, FB, D], U8)
        w0_diff = sb("w0_diff", [P, F], F16)
        w0 = sb("w0", [P, F], F16)
        w1 = sb("w1", [P, FB, F], F16)
        w2 = sb("w2", [P, FB, D], F16)
        wqkv = sb("wqkv", [P, 3, D], F32)
        cols = sb("cols", [P, 6], F32)
        bias_q, bias_k, bias_v = (cols[:, i:i + 1] for i in range(3))
        tap_prev, tap_mid, tap_next = (cols[:, i:i + 1] for i in range(3, 6))
        neg_tap_next = sb("neg_tap_next", [P, 1], F32)
        s_cols = sb("s_cols", [P, 3], F32)
        s_pos = sb("s_pos", [P, 2], F32)
        s_neg = sb("s_neg", [P, 2], F32)
        s_sign = sb("s_sign", [P, 2], F32)
        s_abs = sb("s_abs", [P, 2], F32)
        w1_mul = sb("w1_mul", [P, 1], F32)
        w1_add = sb("w1_add", [P, 1], F32)
        ffn_fac_a = sb("ffn_fac_a", [P, 1], F32)
        ffn_fac = sb("ffn_fac", [P, 1], F32)
        warm = sb("warm", [P, 512], BF16)
        zeros = sb("zeros", [P, P], F32)
        ident = sb("ident", [P, P], F32)
        ident_bf = sb("ident_bf", [P, P], BF16)
        mask_bf = sb("mask_bf", [P, P], BF16)
        neg_half = sb("neg_half", [P, T], F32)
        eps = sb("eps", [P, T], F32)

        def per_slot(name, shape, dt, count=2):
            return [sb(f"{name}{k}", shape, dt) for k in range(count)]

        ln_stats = per_slot("ln_stats", [P, T, 6], F32, SLOTS)
        ln_mv = per_slot("ln_mv", [P, T, 2], F32, SLOTS)
        ln_var = per_slot("ln_var", [P, T], F32, SLOTS)
        ln_rstd = per_slot("ln_rstd", [P, T], F32, SLOTS)
        xn = per_slot("xn", [P, T, D], F32, SLOTS)
        xt_hi, xt_lo = per_slot("xt_hi", [P, S], F16), per_slot("xt_lo", [P, S], F16)
        h1_hi, h1_lo = per_slot("h1_hi", [P, FB, S], F16), per_slot("h1_lo", [P, FB, S], F16)
        h2_hi, h2_lo = per_slot("h2_hi", [P, FB, S], F16), per_slot("h2_lo", [P, FB, S], F16)
        xt_attn = per_slot("xt_attn", [P, S], F32)
        q_t, k_t = per_slot("q_t", [P, S], F32), per_slot("k_t", [P, S], F32)
        v_t = per_slot("v_t", [P, S + 2], F32)
        next_t = per_slot("next_t", [P, S], F32)
        mid_t, prev_t = per_slot("mid_t", [P, S], F32), per_slot("prev_t", [P, S], F32)
        pm_t, conv_t = per_slot("pm_t", [P, S], F32), per_slot("conv_t", [P, S], F32)
        conv_next = per_slot("conv_next", [P, 2 * T, D], F32)
        neg_max = per_slot("neg_max", [P, T], F32)
        prob = per_slot("prob", [P, 3, P], F32)
        prob_sum, prob_inv = per_slot("prob_sum", [P, T], F32), per_slot("prob_inv", [P, T], F32)
        prob_t = per_slot("prob_t", [P, 3, P], F32)
        diag_block = per_slot("diag_block", [P, T, P], F32)
        prob_diag = per_slot("prob_diag", [P, T], F32)
        diag_weight = per_slot("diag_weight", [P, T], F32)
        diag_term = per_slot("diag_term", [P, T, D], F32)

        ps_ffn = [ctx.enter_context(nc.psum_tensor(f"ps_ffn{k}", [P, 2, 512], F32)) for k in range(2)]
        ps_attn = [ctx.enter_context(nc.psum_tensor(f"ps_attn{k}", [P, 2, 512], F32)) for k in range(2)]

        scalars_loaded, cols_loaded = sem("scalars_loaded"), sem("cols_loaded")
        k0_loaded, k1_loaded, k2_loaded = sem("k0_loaded"), sem("k1_loaded"), sem("k2_loaded")
        wqkv_loaded = sem("wqkv_loaded")
        X_PARTS = [(0, 1), (1, 2), (2, 4), (4, B)]
        x_loaded = [sem(f"x_loaded{i}") for i in range(len(X_PARTS))]
        warm_ready = sem("warm_ready")
        consts_step = sem("consts_step")
        consts_ready = sem("consts_ready")
        scal_step = sem("scal_step")
        scal_ready, fac_ready = sem("scal_ready"), sem("fac_ready")
        w0_step, w0_ready, w1_ready, w2_ready = sem("w0_step"), sem("w0_ready"), sem("w1_ready"), sem("w2_ready")
        stored = sem("stored")

        def per_slot_sem(name, count=2):
            return [sem(f"{name}{k}") for k in range(count)]

        stats_done = per_slot_sem("stats_done", SLOTS)
        mv_done = per_slot_sem("mv_done", SLOTS)
        var_done = per_slot_sem("var_done", SLOTS)
        rstd_done = per_slot_sem("rstd_done", SLOTS)
        xn_ready = per_slot_sem("xn_ready", SLOTS)
        xt_done = per_slot_sem("xt_done", SLOTS)
        added = per_slot_sem("added", SLOTS)

        xt_hi_ready, xt_lo_ready = per_slot_sem("xt_hi_ready"), per_slot_sem("xt_lo_ready")
        l1_done, l2_done = per_slot_sem("l1_done"), per_slot_sem("l2_done")
        h1_hi_ready, h1_lo_ready = per_slot_sem("h1_hi_ready"), per_slot_sem("h1_lo_ready")
        h2_hi_ready, h2_lo_ready = per_slot_sem("h2_hi_ready"), per_slot_sem("h2_lo_ready")
        l3_done = per_slot_sem("l3_done")

        xt_attn_ready = per_slot_sem("xt_attn_ready")
        q_done, kv_done = per_slot_sem("q_done"), per_slot_sem("kv_done")
        q_ready, k_ready, v_ready = per_slot_sem("q_ready"), per_slot_sem("k_ready"), per_slot_sem("v_ready")
        taps_done = per_slot_sem("taps_done")
        pm_done, conv_ready = per_slot_sem("pm_done"), per_slot_sem("conv_ready")
        scores_done = per_slot_sem("scores_done")
        max_ready = per_slot_sem("max_ready")
        probs_ready = per_slot_sem("probs_ready")
        diag_done = per_slot_sem("diag_done")
        inv_ready, diag_weight_ready = per_slot_sem("inv_ready"), per_slot_sem("diag_weight_ready")
        diag_term_done = per_slot_sem("diag_term_done")
        diag_added = per_slot_sem("diag_added")
        conv_next_done, conv_next_ready = per_slot_sem("conv_next_done"), per_slot_sem("conv_next_ready")
        prob_t_done, prob_t_ready = per_slot_sem("prob_t_done"), per_slot_sem("prob_t_ready")
        attn_out_done = per_slot_sem("attn_out_done")

        def ffn1(b):
            return (b, 0, b) if isinstance(b, int) and b < 2 else (0, b - 1, b)

        def ffn2(b):
            return (b - (B - 2), B - 1, b) if isinstance(b, int) and b >= B - 2 else (1, b + 1, b)

        def attn(b):
            return (ATTN + 1, 0, b) if isinstance(b, int) and b == B - 1 else (ATTN, b, b)

        def after_first(n):
            return not isinstance(n, int) or n > 0

        LOOP_FROM, LOOP_TO = 4, B

        block = ctx.enter_context(nc.Block())

        @block.sync
        def _(sp):
            def load_x(part):
                a, z = X_PARTS[part]
                sp.dma_start(x_sb[:, a:z], x[a:z].rearrange("b (t p) d -> p b t d", p=P)).then_inc(x_loaded[part], 16)

            def store(b):
                sp.dma_start(out[b].rearrange("(t p) d -> p t d", p=P), x_sb[:, b]).then_inc(stored, 16)

            load_x(0)
            sp.dma_start(k0_u8[:], k0.rearrange("(c p) f -> p c f", p=P)).then_inc(k0_loaded, 16)
            load_x(1)
            sp.dma_start(wqkv[:], w_qkv.rearrange("p (c d) -> p c d", c=3)).then_inc(wqkv_loaded, 16)
            load_x(2)
            load_x(3)
            with sp.Fori(0, B - 2) as b:
                sp.wait_ge(added[1], b + 2)
                store(b)
            for b in range(B - 2, B):
                slot, n, _ = ffn2(b)
                sp.wait_ge(added[slot], n + 1)
                store(b)
            sp.wait_ge(stored, 16 * B)

        @block.gpsimd
        def _(pool):
            nc.gpsimd.memset(zeros[:], 0.0).then_inc(consts_step, 1)
            nc.gpsimd.memset(neg_half[:], -0.5).then_inc(consts_step, 1)
            nc.gpsimd.memset(eps[:], LN_EPS).then_inc(consts_step, 1)
            for a in range(2):
                nc.gpsimd.memset(v_t[a][:, 0:1], 0.0).then_inc(consts_step, 1)
                nc.gpsimd.memset(v_t[a][:, S + 1:S + 2], 0.0).then_inc(consts_step, 1)
            pool.wait_ge(consts_step, 7)
            for dst, compare, fill in ((ident, ALU.not_equal, 1.0), (ident_bf, ALU.not_equal, 1.0), (mask_bf, ALU.is_ge, MASKED)):
                nc.gpsimd.affine_select(out=dst[:], in_=zeros[:], compare_op=compare, fill=fill, base=0,
                                        pattern=[[-1, P]], channel_multiplier=1).then_inc(consts_ready, 1)

            def rstd(job):
                k, n, _ = job
                pool.wait_ge(mv_done[k], T * (n + 1))
                nc.gpsimd.tensor_tensor(ln_var[k][:], ln_mv[k][:, :, 1], eps[:], ALU.add).then_inc(var_done[k], 1)
                pool.wait_ge(var_done[k], n + 1)
                nc.gpsimd.tensor_tensor(ln_rstd[k][:], ln_var[k][:], neg_half[:], ALU.pow).then_inc(rstd_done[k], 1)

            def conv_values(job):
                a, n = job[0] - ATTN, job[1]
                pool.wait_ge(v_ready[a], n + 1)
                for shift, (dst, tap) in enumerate(((prev_t, tap_prev), (mid_t, tap_mid), (next_t, neg_tap_next[:]))):
                    nc.gpsimd.tensor_tensor(dst[a][:], v_t[a][:, shift:shift + S], tap.to_broadcast([P, S]),
                                            ALU.mult).then_inc(taps_done[a], 1)
                pool.wait_ge(taps_done[a], 3 * (n + 1))
                nc.gpsimd.tensor_tensor(pm_t[a][:], prev_t[a][:], mid_t[a][:], ALU.add).then_inc(pm_done[a], 1)
                pool.wait_ge(pm_done[a], n + 1)
                nc.gpsimd.tensor_tensor(conv_t[a][:], pm_t[a][:], next_t[a][:], ALU.subtract).then_inc(conv_ready[a], 1)

            def add_diagonal(job):
                a, n, b = job[0] - ATTN, job[1], job[2]
                pool.wait_ge(conv_next_ready[a], n + 1)
                pool.wait_ge(diag_weight_ready[a], n + 1)
                nc.gpsimd.tensor_tensor(diag_term[a][:], conv_next[a][:, T:2 * T],
                                        diag_weight[a][:].unsqueeze(2).to_broadcast([P, T, D]), ALU.mult).then_inc(diag_term_done[a], 1)
                pool.wait_ge(diag_term_done[a], n + 1)
                nc.gpsimd.tensor_tensor(x_sb[:, b], x_sb[:, b], diag_term[a][:], ALU.add).then_inc(diag_added[a], 1)

            rstd(ffn1(0))
            rstd(ffn1(1))
            pool.wait_ge(cols_loaded, 16)
            nc.gpsimd.tensor_scalar(neg_tap_next[:], tap_next, -1.0, 1.0, ALU.mult, ALU.mult).then_inc(consts_step, 1)
            rstd(ffn1(2))
            rstd(attn(0))
            pool.wait_ge(consts_step, 8)
            conv_values(attn(0))
            rstd(ffn1(3))
            add_diagonal(attn(0))
            rstd(attn(1))
            rstd(ffn2(0))

            def iteration(t, last=False):
                conv_values(attn(t - 2))
                if not last:
                    rstd(ffn1(t + 1))
                add_diagonal(attn(t - 2))
                rstd(attn(t - 1))
                rstd(ffn2(t - 2))

            iteration(LOOP_FROM - 1)
            with pool.Fori(LOOP_FROM, LOOP_TO - 1) as t:
                iteration(t)
            iteration(LOOP_TO - 1, last=True)

            rstd(attn(B - 1))
            conv_values(attn(B - 2))
            conv_values(attn(B - 1))
            add_diagonal(attn(B - 2))
            rstd(ffn2(B - 2))
            add_diagonal(attn(B - 1))
            rstd(ffn2(B - 1))

        @block.scalar
        def _(act):
            act.dma_start(s_cols[:], scalars.partition_broadcast(P)).then_inc(scalars_loaded, 16)
            act.dma_start(k1_u8[:], k1.rearrange("(c p) f -> p c f", p=P)).then_inc(k1_loaded, 16)
            act.dma_start(k2_u8[:], k2.rearrange("(c p) f -> p c f", p=P)).then_inc(k2_loaded, 16)
            act.dma_start(cols[:], attn_cols).then_inc(cols_loaded, 16)
            nc.scalar.preload_act_table(ACT.Exp)

            def split_hi_xt(job):
                s, n, _ = job
                act.wait_ge(xt_done[s], n + 1)
                nc.scalar.activation(xt_hi[s][:], ps_ffn[s][:, 1, 0:S], ACT.Copy, scale=XN_SCALE).then_inc(xt_hi_ready[s], 1)

            def split_hi(job, half, done, hi, ready):
                s, n, _ = job
                act.wait_ge(done[s], 2 * n + half + 1)
                nc.scalar.activation(hi[s][:, HALF * half:HALF * half + HALF], ps_ffn[s][:, half], ACT.Relu).then_inc(ready[s], 1)

            def h1_hi_half(job, half):
                split_hi(job, half, l1_done, h1_hi, h1_hi_ready)

            def h2_hi_half(job, half):
                split_hi(job, half, l2_done, h2_hi, h2_hi_ready)

            def copy_xt(job):
                a, n = job[0] - ATTN, job[1]
                act.wait_ge(xt_done[ATTN + a], n + 1)
                nc.scalar.copy(xt_attn[a][:], ps_attn[a][:, 0, 0:S]).then_inc(xt_attn_ready[a], 1)

            def kv_bias(job):
                a, n = job[0] - ATTN, job[1]
                act.wait_ge(kv_done[a], n + 1)
                nc.scalar.activation(k_t[a][:], ps_attn[a][:, 1, 0:S], ACT.Identity, bias=bias_k).then_inc(k_ready[a], 1)
                if after_first(n):
                    act.wait_ge(conv_ready[a], n)
                nc.scalar.activation(v_t[a][:, 1:S + 1], ps_attn[a][:, 1, S:2 * S], ACT.Identity, bias=bias_v).then_inc(v_ready[a], 1)

            def softmax_exp(job):
                a, n = job[0] - ATTN, job[1]
                act.wait_ge(max_ready[a], T * (n + 1))
                nc.scalar.activation(prob[a][:, 0], ps_attn[a][:, 1, 0:P], ACT.Exp, bias=neg_max[a][:, 0:1],
                                     accum_out=prob_sum[a][:, 0:1]).then_inc(probs_ready[a], 1)
                nc.scalar.activation(prob[a][:, 1:3], ps_attn[a][:, 1, P:3 * P], ACT.Exp, bias=neg_max[a][:, 1:2],
                                     accum_out=prob_sum[a][:, 1:2]).then_inc(probs_ready[a], 1)

            def copy_conv_next(job):
                a, n = job[0] - ATTN, job[1]
                act.wait_ge(conv_next_done[a], n + 1)
                nc.scalar.copy(conv_next[a][:], ps_attn[a][:, 0]).then_inc(conv_next_ready[a], 1)

            def copy_prob_t(job):
                a, n = job[0] - ATTN, job[1]
                act.wait_ge(prob_t_done[a], n + 1)
                nc.scalar.copy(prob_t[a][:], ps_attn[a][:, 1, 0:3 * P]).then_inc(prob_t_ready[a], 1)

            def make_w1(first, count):
                nc.scalar.activation(w1[:, first:first + count], k1_u8[:, first:first + count], ACT.Identity,
                                     bias=w1_add[:], scale=w1_mul[:]).then_inc(w1_ready, 1)

            act.wait_ge(scal_ready, 1)
            act.wait_ge(k1_loaded, 16)
            make_w1(0, HALF)
            split_hi_xt(ffn1(0))
            make_w1(HALF, HALF)
            split_hi_xt(ffn1(1))
            h1_hi_half(ffn1(0), 0)
            h1_hi_half(ffn1(0), 1)
            h1_hi_half(ffn1(1), 0)
            h1_hi_half(ffn1(1), 1)
            h2_hi_half(ffn1(0), 0)
            h2_hi_half(ffn1(0), 1)
            h2_hi_half(ffn1(1), 0)
            h2_hi_half(ffn1(1), 1)
            split_hi_xt(ffn1(2))
            h1_hi_half(ffn1(2), 0)
            h1_hi_half(ffn1(2), 1)
            act.wait_ge(cols_loaded, 16)
            act.wait_ge(consts_step, 7)
            copy_xt(attn(0))
            kv_bias(attn(0))
            h2_hi_half(ffn1(2), 0)
            softmax_exp(attn(0))
            h2_hi_half(ffn1(2), 1)
            copy_conv_next(attn(0))
            copy_prob_t(attn(0))
            split_hi_xt(ffn1(3))

            def iteration(t, first=False, last=False):
                one, att, two = ffn1(t), attn(t - 2), ffn2(t - 3)
                if not first:
                    h2_hi_half(ffn2(t - 4), 1)
                h1_hi_half(one, 0)
                h1_hi_half(one, 1)
                copy_xt(att)
                kv_bias(att)
                h2_hi_half(one, 0)
                split_hi_xt(two)
                softmax_exp(att)
                h2_hi_half(one, 1)
                h1_hi_half(two, 0)
                h1_hi_half(two, 1)
                copy_conv_next(att)
                copy_prob_t(att)
                h2_hi_half(two, 0)
                if not last:
                    split_hi_xt(ffn1(t + 1))

            iteration(LOOP_FROM - 1, first=True)
            with act.Fori(LOOP_FROM, LOOP_TO - 1) as t:
                iteration(t)
            iteration(LOOP_TO - 1, last=True)

            a0, a1, two = attn(B - 2), attn(B - 1), ffn2(B - 3)
            h2_hi_half(ffn2(B - 4), 1)
            copy_xt(a0)
            copy_xt(a1)
            kv_bias(a0)
            split_hi_xt(two)
            kv_bias(a1)
            h1_hi_half(two, 0)
            h1_hi_half(two, 1)
            softmax_exp(a0)
            h2_hi_half(two, 0)
            softmax_exp(a1)
            copy_conv_next(a0)
            copy_prob_t(a0)
            h2_hi_half(two, 1)
            copy_conv_next(a1)
            copy_prob_t(a1)
            f0, f1 = ffn2(B - 2), ffn2(B - 1)
            split_hi_xt(f0)
            h1_hi_half(f0, 0)
            h1_hi_half(f0, 1)
            split_hi_xt(f1)
            h2_hi_half(f0, 0)
            h1_hi_half(f1, 0)
            h1_hi_half(f1, 1)
            h2_hi_half(f0, 1)
            h2_hi_half(f1, 0)
            h2_hi_half(f1, 1)

        @block.vector
        def _(dve):
            def wait_apart(semaphore, value):
                if not isinstance(value, int):
                    dve.to_reg(value)
                dve.wait_ge(scalars_loaded, 16)
                dve.wait_ge(semaphore, value)

            def ln_moments(job, source):
                k, n, b = job
                if source is None:
                    part = next(i for i, (_, z) in enumerate(X_PARTS) if b < z) if isinstance(b, int) else len(X_PARTS) - 1
                    dve.wait_ge(x_loaded[part], 16)
                else:
                    wait_apart(added[source[0]], source[1] + 1)
                for i in range(T):
                    nc.vector.bn_stats(ln_stats[k][:, i], x_sb[:, b, i]).then_inc(stats_done[k], 1)
                wait_apart(stats_done[k], T * (n + 1))
                for i in range(T):
                    nc.vector.bn_aggr(ln_mv[k][:, i], ln_stats[k][:, i]).then_inc(mv_done[k], 1)

            def ln_apply(job):
                k, n, b = job
                dve.wait_ge(rstd_done[k], n + 1)
                if after_first(n):
                    dve.wait_ge(xt_done[k], n)
                for i in range(T):
                    last = nc.vector.tensor_scalar(xn[k][:, i], x_sb[:, b, i], ln_mv[k][:, i, 0:1],
                                                   ln_rstd[k][:, i:i + 1], ALU.subtract, ALU.mult)
                last.then_inc(xn_ready[k], 1)

            def split_lo_xt(job):
                s, n, _ = job
                dve.wait_ge(xt_hi_ready[s], n + 1)
                nc.vector.scalar_tensor_tensor(out=xt_lo[s][:], in0=ps_ffn[s][:, 1, 0:S], scalar=XN_SCALE, in1=xt_hi[s][:],
                                               op0=ALU.mult, op1=ALU.subtract).then_inc(xt_lo_ready[s], 1)

            def split_lo(job, half, hi, lo, hi_ready, lo_ready):
                s, n, _ = job
                dve.wait_ge(hi_ready[s], 2 * n + half + 1)
                blocks = slice(HALF * half, HALF * half + HALF)
                nc.vector.scalar_tensor_tensor(out=lo[s][:, blocks], in0=ps_ffn[s][:, half], scalar=0.0, in1=hi[s][:, blocks],
                                               op0=ALU.max, op1=ALU.subtract).then_inc(lo_ready[s], 1)

            def h1_lo_half(job, half):
                split_lo(job, half, h1_hi, h1_lo, h1_hi_ready, h1_lo_ready)

            def h2_lo_half(job, half):
                split_lo(job, half, h2_hi, h2_lo, h2_hi_ready, h2_lo_ready)

            def ffn_residual(job):
                s, n, b = job
                dve.wait_ge(l3_done[s], n + 1)
                nc.vector.scalar_tensor_tensor(out=x_sb[:, b], in0=ps_ffn[s][:, 0, 0:T * D], scalar=ffn_fac[:], in1=x_sb[:, b],
                                               op0=ALU.mult, op1=ALU.add).then_inc(added[s], 1)

            def q_bias_scale(job):
                a, n = job[0] - ATTN, job[1]
                dve.wait_ge(q_done[a], n + 1)
                nc.vector.tensor_scalar(q_t[a][:], ps_attn[a][:, 0, 0:S], bias_q, ATTN_SCALE, ALU.add, ALU.mult).then_inc(q_ready[a], 1)

            def softmax_max(job):
                a, n = job[0] - ATTN, job[1]
                dve.wait_ge(scores_done[a], n + 1)
                for i, (lo, hi) in enumerate(((0, P), (P, 3 * P))):
                    nc.vector.tensor_reduce(neg_max[a][:, i:i + 1], ps_attn[a][:, 1, lo:hi], AX_X, ALU.max,
                                            negate=True).then_inc(max_ready[a], 1)

            def softmax_weights(job):
                a, n = job[0] - ATTN, job[1]
                dve.wait_ge(probs_ready[a], T * (n + 1))
                nc.vector.reciprocal(prob_inv[a][:], prob_sum[a][:]).then_inc(inv_ready[a], 1)
                for i in range(T):
                    nc.vector.tensor_tensor_reduce(diag_block[a][:, i], prob[a][:, 2 * i], ident[:], 1.0, 0.0, ALU.mult, ALU.add,
                                                   prob_diag[a][:, i:i + 1]).then_inc(diag_done[a], 1)
                dve.wait_ge(inv_ready[a], n + 1)
                dve.wait_ge(diag_done[a], T * (n + 1))
                nc.vector.tensor_tensor(diag_weight[a][:], prob_diag[a][:], prob_inv[a][:], ALU.mult).then_inc(diag_weight_ready[a], 1)

            def attn_residual(job):
                a, n, b = job[0] - ATTN, job[1], job[2]
                dve.wait_ge(diag_added[a], n + 1)
                dve.wait_ge(attn_out_done[a], n + 1)
                for i in range(T):
                    last = nc.vector.scalar_tensor_tensor(out=x_sb[:, b, i], in0=ps_attn[a][:, 0, i * D:(i + 1) * D],
                                                          scalar=prob_inv[a][:, i:i + 1], in1=x_sb[:, b, i],
                                                          op0=ALU.mult, op1=ALU.add)
                last.then_inc(added[ATTN + a], 1)

            nc.vector.memset(warm[:], 0.0).then_inc(warm_ready, 1)
            dve.wait_ge(scalars_loaded, 16)
            nc.vector.tensor_scalar(s_pos[:], s_cols[:, 0:2], 0.0, None, ALU.is_gt).then_inc(scal_step, 1)
            nc.vector.tensor_scalar(s_neg[:], s_cols[:, 0:2], 0.0, None, ALU.is_lt).then_inc(scal_step, 1)
            ln_moments(ffn1(0), None)
            dve.wait_ge(scal_step, 2)
            nc.vector.tensor_tensor(s_sign[:], s_pos[:], s_neg[:], ALU.subtract).then_inc(scal_step, 1)
            dve.wait_ge(scal_step, 3)
            nc.vector.tensor_scalar(w1_mul[:], s_sign[:, 1:2], 2.0 * W1_SCALE, None, ALU.mult)
            nc.vector.tensor_scalar(w1_add[:], s_sign[:, 1:2], -W1_SCALE, None, ALU.mult).then_inc(scal_ready, 1)
            dve.wait_ge(k0_loaded, 16)
            nc.vector.tensor_tensor(w0_diff[:], k0_u8[:, 0], k0_u8[:, 1], ALU.subtract).then_inc(w0_step, 1)
            ln_apply(ffn1(0))
            dve.wait_ge(w0_step, 1)
            nc.vector.tensor_scalar(w0[:], w0_diff[:], s_sign[:, 0:1], None, ALU.mult).then_inc(w0_ready, 1)
            ln_moments(ffn1(1), None)
            nc.vector.tensor_tensor(s_abs[:], s_cols[:, 0:2], s_sign[:], ALU.mult).then_inc(scal_step, 1)
            split_lo_xt(ffn1(0))
            dve.wait_ge(scal_step, 4)
            nc.vector.tensor_tensor(ffn_fac_a[:], s_abs[:, 0:1], s_abs[:, 1:2], ALU.mult).then_inc(scal_step, 1)
            ln_apply(ffn1(1))
            dve.wait_ge(scal_step, 5)
            nc.vector.scalar_tensor_tensor(out=ffn_fac[:], in0=ffn_fac_a[:], scalar=FINAL_SCALE, in1=s_cols[:, 2:3],
                                           op0=ALU.mult, op1=ALU.mult).then_inc(fac_ready, 1)
            h1_lo_half(ffn1(0), 0)
            split_lo_xt(ffn1(1))
            h1_lo_half(ffn1(0), 1)
            h1_lo_half(ffn1(1), 0)
            h1_lo_half(ffn1(1), 1)
            dve.wait_ge(k2_loaded, 16)
            nc.vector.tensor_scalar(w2[:], k2_u8[:], 2.0, -1.0, ALU.mult, ALU.add).then_inc(w2_ready, 1)
            ln_moments(ffn1(2), None)
            h2_lo_half(ffn1(0), 0)
            ln_apply(ffn1(2))
            h2_lo_half(ffn1(0), 1)
            h2_lo_half(ffn1(1), 0)
            dve.wait_ge(fac_ready, 1)
            ffn_residual(ffn1(0))
            ln_moments(attn(0), ffn1(0))
            h2_lo_half(ffn1(1), 1)
            split_lo_xt(ffn1(2))
            ln_apply(attn(0))
            h1_lo_half(ffn1(2), 0)
            h1_lo_half(ffn1(2), 1)
            ffn_residual(ffn1(1))
            dve.wait_ge(cols_loaded, 16)
            dve.wait_ge(consts_ready, 3)
            q_bias_scale(attn(0))
            ln_moments(ffn1(3), None)
            h2_lo_half(ffn1(2), 0)
            softmax_max(attn(0))
            ln_apply(ffn1(3))
            softmax_weights(attn(0))
            h2_lo_half(ffn1(2), 1)
            ln_moments(attn(1), ffn1(1))
            ffn_residual(ffn1(2))
            ln_apply(attn(1))
            attn_residual(attn(0))
            ln_moments(ffn2(0), attn(0))
            split_lo_xt(ffn1(3))

            def iteration(t, first=False, last=False):
                one, att, two = ffn1(t), attn(t - 2), ffn2(t - 3)
                if not first:
                    h2_lo_half(ffn2(t - 4), 1)
                h1_lo_half(one, 0)
                h1_lo_half(one, 1)
                ln_apply(two)
                if not first:
                    ffn_residual(ffn2(t - 4))
                q_bias_scale(att)
                if not last:
                    ln_moments(ffn1(t + 1), None)
                h2_lo_half(one, 0)
                split_lo_xt(two)
                softmax_max(att)
                if not last:
                    ln_apply(ffn1(t + 1))
                softmax_weights(att)
                h2_lo_half(one, 1)
                h1_lo_half(two, 0)
                h1_lo_half(two, 1)
                ln_moments(attn(t - 1), ffn1(t - 1))
                ffn_residual(one)
                attn_residual(att)
                ln_moments(ffn2(t - 2), att)
                ln_apply(attn(t - 1))
                h2_lo_half(two, 0)
                if not last:
                    split_lo_xt(ffn1(t + 1))

            iteration(LOOP_FROM - 1, first=True)
            with dve.Fori(LOOP_FROM, LOOP_TO - 1) as t:
                iteration(t)
            iteration(LOOP_TO - 1, last=True)

            a0, a1, two = attn(B - 2), attn(B - 1), ffn2(B - 3)
            ln_moments(a1, ffn1(B - 1))
            h2_lo_half(ffn2(B - 4), 1)
            ln_apply(a1)
            ln_apply(two)
            q_bias_scale(a0)
            ffn_residual(ffn2(B - 4))
            split_lo_xt(two)
            q_bias_scale(a1)
            h1_lo_half(two, 0)
            h1_lo_half(two, 1)
            softmax_max(a0)
            softmax_weights(a0)
            h2_lo_half(two, 0)
            softmax_max(a1)
            softmax_weights(a1)
            h2_lo_half(two, 1)
            attn_residual(a0)
            ln_moments(ffn2(B - 2), a0)
            ln_apply(ffn2(B - 2))
            ffn_residual(two)
            f0, f1 = ffn2(B - 2), ffn2(B - 1)
            attn_residual(a1)
            ln_moments(f1, a1)
            split_lo_xt(f0)
            ln_apply(f1)
            h1_lo_half(f0, 0)
            h1_lo_half(f0, 1)
            split_lo_xt(f1)
            h2_lo_half(f0, 0)
            h1_lo_half(f1, 0)
            h1_lo_half(f1, 1)
            h2_lo_half(f0, 1)
            h2_lo_half(f1, 0)
            ffn_residual(f0)
            h2_lo_half(f1, 1)
            ffn_residual(f1)

        @block.tensor
        def _(pe):
            def transpose_rows(job):
                k, n, _ = job
                ps, bank = (ps_attn[k - ATTN], 0) if k >= ATTN else (ps_ffn[k], 1)
                pe.wait_ge(xn_ready[k], n + 1)
                if k >= ATTN and after_first(n):
                    pe.wait_ge(added[k], n)
                for i in range(T):
                    last = nc.tensor.transpose(ps[:, bank, i * P:(i + 1) * P], xn[k][:, i], ident[:])
                last.then_inc(xt_done[k], 1)

            def layer1(job):
                s, n, _ = job
                pe.wait_ge(xt_lo_ready[s], n + 1)
                if after_first(n):
                    pe.wait_ge(added[s], n)
                for half in range(2):
                    for c in range(HALF):
                        block_out = HALF * half + c
                        w = w0[:, block_out * P:(block_out + 1) * P]
                        dst = ps_ffn[s][:, half, c * S:(c + 1) * S]
                        nc.tensor.matmul(dst, w, xt_hi[s][:], start=True, stop=False)
                        last = nc.tensor.matmul(dst, w, xt_lo[s][:], start=False, stop=True)
                    last.then_inc(l1_done[s], 1)

            def layer2_half(job, half):
                s, n, _ = job
                for c in range(HALF):
                    block_out = HALF * half + c
                    dst = ps_ffn[s][:, half, c * S:(c + 1) * S]
                    for j in range(FB):
                        if half == 0 and c == 0 and j % HALF == 0:
                            pe.wait_ge(h1_lo_ready[s], 2 * n + j // HALF + 1)
                        w = w1[:, j, block_out * P:(block_out + 1) * P]
                        nc.tensor.matmul(dst, w, h1_hi[s][:, j], start=(j == 0), stop=False)
                        last = nc.tensor.matmul(dst, w, h1_lo[s][:, j], start=False, stop=(j == FB - 1))
                last.then_inc(l2_done[s], 1)

            def layer3(job):
                s, n, _ = job
                pe.wait_ge(h2_lo_ready[s], 2 * (n + 1))
                for i in range(T):
                    for j in range(FB):
                        rows = slice(i * P, (i + 1) * P)
                        dst = ps_ffn[s][:, 0, i * D:(i + 1) * D]
                        nc.tensor.matmul(dst, h2_hi[s][:, j, rows], w2[:, j], start=(j == 0), stop=False)
                        last = nc.tensor.matmul(dst, h2_lo[s][:, j, rows], w2[:, j], start=False, stop=(j == FB - 1))
                last.then_inc(l3_done[s], 1)

            def project_qkv(job):
                a, n = job[0] - ATTN, job[1]
                pe.wait_ge(xt_attn_ready[a], n + 1)
                nc.tensor.matmul(ps_attn[a][:, 1, 0:S], wqkv[:, 1], xt_attn[a][:], start=True, stop=True)
                nc.tensor.matmul(ps_attn[a][:, 1, S:2 * S], wqkv[:, 2], xt_attn[a][:], start=True, stop=True).then_inc(kv_done[a], 1)
                nc.tensor.matmul(ps_attn[a][:, 0, 0:S], wqkv[:, 0], xt_attn[a][:], start=True, stop=True).then_inc(q_done[a], 1)

            def scores(job):
                a, n = job[0] - ATTN, job[1]
                ps = ps_attn[a]
                pe.wait_ge(q_ready[a], n + 1)
                pe.wait_ge(k_ready[a], n + 1)
                pe.wait_ge(v_ready[a], n + 1)
                nc.tensor.matmul(ps[:, 1, 0:P], q_t[a][:, 0:P], k_t[a][:, 0:P], start=True, stop=False)
                nc.tensor.matmul(ps[:, 1, 0:P], ident_bf[:], mask_bf[:], start=False, stop=True)
                nc.tensor.matmul(ps[:, 1, P:3 * P], q_t[a][:, P:S], k_t[a][:], start=True, stop=False, skip_group_check=True)
                nc.tensor.matmul(ps[:, 1, 2 * P:3 * P], ident_bf[:], mask_bf[:], start=False, stop=True,
                                 skip_group_check=True).then_inc(scores_done[a], 1)

            def transpose_conv(job):
                a, n = job[0] - ATTN, job[1]
                pe.wait_ge(conv_ready[a], n + 1)
                for m, src in enumerate((conv_t, next_t)):
                    for i in range(T):
                        last = nc.tensor.transpose(ps_attn[a][:, 0, (T * m + i) * P:(T * m + i + 1) * P],
                                                   src[a][:, i * P:(i + 1) * P], ident[:])
                last.then_inc(conv_next_done[a], 1)

            def transpose_probs(job):
                a, n = job[0] - ATTN, job[1]
                pe.wait_ge(probs_ready[a], T * (n + 1))
                for m in range(3):
                    last = nc.tensor.transpose(ps_attn[a][:, 1, m * P:(m + 1) * P], prob[a][:, m], ident[:])
                last.then_inc(prob_t_done[a], 1)

            def attend(job):
                a, n = job[0] - ATTN, job[1]
                pe.wait_ge(conv_next_ready[a], n + 1)
                pe.wait_ge(prob_t_ready[a], n + 1)
                for i in range(T):
                    for j in range(i + 1):
                        last = nc.tensor.matmul(ps_attn[a][:, 0, i * D:(i + 1) * D], prob_t[a][:, i + j], conv_next[a][:, j],
                                                start=(j == 0), stop=(j == i))
                last.then_inc(attn_out_done[a], 1)

            pe.wait_ge(warm_ready, 1)
            for _ in range(WARM_UP):
                nc.tensor.matmul(ps_attn[1][:, 0], warm[:, 0:P], warm[:], start=True, stop=True)
            pe.wait_ge(consts_ready, 3)
            transpose_rows(ffn1(0))
            pe.wait_ge(w0_ready, 1)
            layer1(ffn1(0))
            transpose_rows(ffn1(1))
            layer1(ffn1(1))
            pe.wait_ge(w1_ready, 2)
            layer2_half(ffn1(0), 0)
            layer2_half(ffn1(0), 1)
            layer2_half(ffn1(1), 0)
            pe.wait_ge(w2_ready, 1)
            layer3(ffn1(0))
            layer2_half(ffn1(1), 1)
            transpose_rows(ffn1(2))
            layer1(ffn1(2))
            layer3(ffn1(1))
            transpose_rows(attn(0))
            pe.wait_ge(wqkv_loaded, 16)
            project_qkv(attn(0))
            layer2_half(ffn1(2), 0)
            scores(attn(0))
            layer2_half(ffn1(2), 1)
            transpose_conv(attn(0))
            transpose_probs(attn(0))
            layer3(ffn1(2))
            attend(attn(0))
            transpose_rows(ffn1(3))

            def iteration(t, first=False, last=False):
                one, att, two = ffn1(t), attn(t - 2), ffn2(t - 3)
                layer1(one)
                transpose_rows(att)
                if not first:
                    layer3(ffn2(t - 4))
                project_qkv(att)
                layer2_half(one, 0)
                transpose_rows(two)
                scores(att)
                layer2_half(one, 1)
                layer1(two)
                transpose_conv(att)
                transpose_probs(att)
                layer3(one)
                attend(att)
                layer2_half(two, 0)
                if not last:
                    transpose_rows(ffn1(t + 1))
                layer2_half(two, 1)

            iteration(LOOP_FROM - 1, first=True)
            with pe.Fori(LOOP_FROM, LOOP_TO - 1) as t:
                iteration(t)
            iteration(LOOP_TO - 1, last=True)

            a0, a1, two = attn(B - 2), attn(B - 1), ffn2(B - 3)
            transpose_rows(a0)
            transpose_rows(a1)
            project_qkv(a0)
            layer3(ffn2(B - 4))
            transpose_rows(two)
            project_qkv(a1)
            layer1(two)
            scores(a0)
            layer2_half(two, 0)
            scores(a1)
            transpose_conv(a0)
            transpose_probs(a0)
            layer2_half(two, 1)
            attend(a0)
            transpose_conv(a1)
            transpose_probs(a1)
            layer3(two)
            attend(a1)
            f0, f1 = ffn2(B - 2), ffn2(B - 1)
            transpose_rows(f0)
            layer1(f0)
            transpose_rows(f1)
            layer2_half(f0, 0)
            layer1(f1)
            layer2_half(f0, 1)
            layer2_half(f1, 0)
            layer3(f0)
            layer2_half(f1, 1)
            layer3(f1)


def kernel(**inputs):
    import numpy as np
    import concourse.bacc as bacc
    from concourse.bass_utils import run_bass_kernel_spmd

    a = {name.split("_", 2)[2]: np.ascontiguousarray(v) for name, v in inputs.items()}
    arrays = {
        "x": a["x"],
        "w_qkv": a["W_qkv"],
        "attn_cols": np.concatenate([a["b_qkv"].reshape(3, -1).T, a["W_vconv"]], axis=1),
        "k0": a["k0"],
        "k1": a["k1"],
        "k2": a["k2"],
        "scalars": np.concatenate([a[s].reshape(1, 1) for s in ("s0", "s1", "s2")], axis=1),
    }
    nc = bacc.Bacc("TRN2", target_bir_lowering=False, num_devices=1)
    args = [nc.dram_tensor(f"in_{name}", v.shape, mybir.dt.from_np(v.dtype), kind="ExternalInput").ap()
            for name, v in arrays.items()]
    out = nc.dram_tensor("out_y", a["x"].shape, F32, kind="ExternalOutput").ap()
    macaron_kernel(nc, *args, out)
    r = run_bass_kernel_spmd(nc, [{f"in_{name}": np.ascontiguousarray(v) for name, v in arrays.items()}], core_ids=[0])
    return r.results[0]["out_y"]
```

```python
from contextlib import ExitStack

import concourse.bass as bass
from concourse import mybir

ALU = mybir.AluOpType
ACT = mybir.ActivationFunctionType
F32 = mybir.dt.float32
F16 = mybir.dt.float16
BF16 = mybir.dt.bfloat16
U8 = mybir.dt.uint8

P = 128
LN_EPS = 1e-5
MASKED = -1e30
WARM_UP, WARM_UP_MORE = 11, 2

SLOTS, ATTN = 4, 2

XN_SCALE = 2.0 ** 6
W1_SCALE = 2.0 ** -7


def macaron_kernel(nc, x, w_qkv, attn_cols, k0, k1, k2, scalars, out):
    B, S, D = x.shape
    F = k1.shape[0]
    T = S // P
    FB = F // P
    HALF = FB // 2
    assert D == P and T == 2 and FB == 4 and k0.shape[0] == 2 * D and B == 8
    ATTN_SCALE = float(D) ** -0.5
    FINAL_SCALE = 0.5 * 2.0 * 2.0 * 2.0 / (XN_SCALE * W1_SCALE)

    with ExitStack() as ctx:
        def sb(name, shape, dt):
            return ctx.enter_context(nc.sbuf_tensor(name, shape, dt))

        def sem(name):
            return ctx.enter_context(nc.semaphore(name))

        x_sb = sb("x_sb", [P, B, T, D], F32)
        k0_u8 = sb("k0_u8", [P, 2, F], U8)
        k1_u8 = sb("k1_u8", [P, FB, F], U8)
        k2_u8 = sb("k2_u8", [P, FB, D], U8)
        w0_diff = sb("w0_diff", [P, F], F16)
        w0 = sb("w0", [P, F], F16)
        w1 = sb("w1", [P, FB, F], F16)
        w2 = sb("w2", [P, FB, D], F16)
        wqkv = sb("wqkv", [P, 3, D], F32)
        cols = sb("cols", [P, 6], F32)
        bias_q, bias_k, bias_v = (cols[:, i:i + 1] for i in range(3))
        tap_prev, tap_mid, tap_next = (cols[:, i:i + 1] for i in range(3, 6))
        neg_tap_next = sb("neg_tap_next", [P, 1], F32)
        scaled_bias_q = sb("scaled_bias_q", [P, 1], F32)
        s_cols = sb("s_cols", [P, 3], F32)
        s_pos = sb("s_pos", [P, 2], F32)
        s_neg = sb("s_neg", [P, 2], F32)
        s_sign = sb("s_sign", [P, 2], F32)
        s_abs = sb("s_abs", [P, 2], F32)
        w1_mul = sb("w1_mul", [P, 1], F32)
        w1_add = sb("w1_add", [P, 1], F32)
        ffn_fac_a = sb("ffn_fac_a", [P, 1], F32)
        ffn_fac = sb("ffn_fac", [P, 1], F32)
        warm = sb("warm", [P, 512], BF16)
        zeros = sb("zeros", [P, 2 * P], F32)
        ident = sb("ident", [P, P], F32)
        mask = sb("mask", [P, 2, P], F32)
        neg_half = sb("neg_half", [P, T], F32)
        eps = sb("eps", [P, T], F32)

        def per_slot(name, shape, dt, count=2):
            return [sb(f"{name}{k}", shape, dt) for k in range(count)]

        ln_stats = per_slot("ln_stats", [P, T, 6], F32, SLOTS)
        ln_mv = per_slot("ln_mv", [P, T, 2], F32, SLOTS)
        ln_var = per_slot("ln_var", [P, T], F32, SLOTS)
        ln_rstd = per_slot("ln_rstd", [P, T], F32, SLOTS)
        xn = per_slot("xn", [P, T, D], F32, SLOTS)
        xt_hi, xt_lo = per_slot("xt_hi", [P, S], F16), per_slot("xt_lo", [P, S], F16)
        h1_hi, h1_lo = per_slot("h1_hi", [P, FB, S], F16), per_slot("h1_lo", [P, FB, S], F16)
        h2_hi, h2_lo = per_slot("h2_hi", [P, FB, S], F16), per_slot("h2_lo", [P, FB, S], F16)
        xt_attn = per_slot("xt_attn", [P, S], F32)
        q_t, k_t = per_slot("q_t", [P, S], F32), per_slot("k_t", [P, S], F32)
        v_t = per_slot("v_t", [P, S + 2], F32)
        next_t = per_slot("next_t", [P, S], F32)
        mid_t, prev_t = per_slot("mid_t", [P, S], F32), per_slot("prev_t", [P, S], F32)
        pm_t, conv_t = per_slot("pm_t", [P, S], F32), per_slot("conv_t", [P, S], F32)
        conv_next = per_slot("conv_next", [P, 2 * T, D], F32)
        neg_scores = per_slot("neg_scores", [P, 3, P], F32)
        neg_max = per_slot("neg_max", [P, T], F32)
        prob = per_slot("prob", [P, 3, P], F32)
        prob_sum, prob_inv = per_slot("prob_sum", [P, T], F32), per_slot("prob_inv", [P, T], F32)
        prob_t = per_slot("prob_t", [P, 3, P], F32)
        diag_block = per_slot("diag_block", [P, T, P], F32)
        prob_diag = per_slot("prob_diag", [P, T], F32)
        diag_weight = per_slot("diag_weight", [P, T], F32)
        diag_term = per_slot("diag_term", [P, T, D], F32)

        ps_ffn = [ctx.enter_context(nc.psum_tensor(f"ps_ffn{k}", [P, 2, 512], F32)) for k in range(2)]
        ps_attn = [ctx.enter_context(nc.psum_tensor(f"ps_attn{k}", [P, 2, 512], F32)) for k in range(2)]

        scalars_loaded, cols_loaded = sem("scalars_loaded"), sem("cols_loaded")
        k0_loaded, k1_loaded, k2_loaded = sem("k0_loaded"), sem("k1_loaded"), sem("k2_loaded")
        wqkv_loaded = sem("wqkv_loaded")
        X_PARTS = [(0, 1), (1, 2), (2, 4), (4, B)]
        x_loaded = [sem(f"x_loaded{i}") for i in range(len(X_PARTS))]
        warm_ready = sem("warm_ready")
        consts_step = sem("consts_step")
        consts_ready = sem("consts_ready")
        scal_step = sem("scal_step")
        scal_ready, fac_ready = sem("scal_ready"), sem("fac_ready")
        w0_step, w0_ready, w1_ready, w2_ready = sem("w0_step"), sem("w0_ready"), sem("w1_ready"), sem("w2_ready")
        stored = sem("stored")

        def per_slot_sem(name, count=2):
            return [sem(f"{name}{k}") for k in range(count)]

        stats_done = per_slot_sem("stats_done", SLOTS)
        mv_done = per_slot_sem("mv_done", SLOTS)
        var_done = per_slot_sem("var_done", SLOTS)
        rstd_done = per_slot_sem("rstd_done", SLOTS)
        xn_ready = per_slot_sem("xn_ready", SLOTS)
        xt_done = per_slot_sem("xt_done", SLOTS)
        added = per_slot_sem("added", SLOTS)

        xt_hi_ready, xt_lo_ready = per_slot_sem("xt_hi_ready"), per_slot_sem("xt_lo_ready")
        l1_done, l2_done = per_slot_sem("l1_done"), per_slot_sem("l2_done")
        h1_hi_ready, h1_lo_ready = per_slot_sem("h1_hi_ready"), per_slot_sem("h1_lo_ready")
        h2_hi_ready, h2_lo_ready = per_slot_sem("h2_hi_ready"), per_slot_sem("h2_lo_ready")
        l3_done = per_slot_sem("l3_done")

        xt_attn_ready = per_slot_sem("xt_attn_ready")
        q_done, kv_done = per_slot_sem("q_done"), per_slot_sem("kv_done")
        q_ready, k_ready, v_ready = per_slot_sem("q_ready"), per_slot_sem("k_ready"), per_slot_sem("v_ready")
        taps_done = per_slot_sem("taps_done")
        pm_done, conv_ready = per_slot_sem("pm_done"), per_slot_sem("conv_ready")
        scores_done = per_slot_sem("scores_done")
        max_ready = per_slot_sem("max_ready")
        probs_ready = per_slot_sem("probs_ready")
        diag_done = per_slot_sem("diag_done")
        inv_ready, diag_weight_ready = per_slot_sem("inv_ready"), per_slot_sem("diag_weight_ready")
        diag_term_done = per_slot_sem("diag_term_done")
        diag_added = per_slot_sem("diag_added")
        conv_next_done, conv_next_ready = per_slot_sem("conv_next_done"), per_slot_sem("conv_next_ready")
        prob_t_done, prob_t_ready = per_slot_sem("prob_t_done"), per_slot_sem("prob_t_ready")
        attn_out_done = per_slot_sem("attn_out_done")

        def ffn1(b):
            return (b, 0, b) if isinstance(b, int) and b < 2 else (0, b - 1, b)

        def ffn2(b):
            return (b - (B - 2), B - 1, b) if isinstance(b, int) and b >= B - 2 else (1, b + 1, b)

        def attn(b):
            return (ATTN + 1, 0, b) if isinstance(b, int) and b == B - 1 else (ATTN, b, b)

        def after_first(n):
            return not isinstance(n, int) or n > 0

        LOOP_FROM, LOOP_TO = 4, B

        block = ctx.enter_context(nc.Block())

        @block.sync
        def _(sp):
            def load_x(part):
                a, z = X_PARTS[part]
                sp.dma_start(x_sb[:, a:z], x[a:z].rearrange("b (t p) d -> p b t d", p=P)).then_inc(x_loaded[part], 16)

            def store(b):
                sp.dma_start(out[b].rearrange("(t p) d -> p t d", p=P), x_sb[:, b]).then_inc(stored, 16)

            load_x(0)
            load_x(1)
            sp.dma_start(s_cols[:], scalars.partition_broadcast(P)).then_inc(scalars_loaded, 16)
            sp.dma_start(k1_u8[:], k1.rearrange("(c p) f -> p c f", p=P)).then_inc(k1_loaded, 16)
            sp.dma_start(k0_u8[:], k0.rearrange("(c p) f -> p c f", p=P)).then_inc(k0_loaded, 16)
            sp.dma_start(cols[:], attn_cols).then_inc(cols_loaded, 16)
            sp.dma_start(k2_u8[:], k2.rearrange("(c p) f -> p c f", p=P)).then_inc(k2_loaded, 16)
            sp.dma_start(wqkv[:], w_qkv.rearrange("p (c d) -> p c d", c=3)).then_inc(wqkv_loaded, 16)
            load_x(2)
            load_x(3)
            with sp.Fori(0, B - 2) as b:
                sp.wait_ge(added[1], b + 2)
                store(b)
            for b in range(B - 2, B):
                slot, n, _ = ffn2(b)
                sp.wait_ge(added[slot], n + 1)
                store(b)
            sp.wait_ge(stored, 16 * B)

        @block.gpsimd
        def _(pool):
            nc.gpsimd.memset(zeros[:], 0.0).then_inc(consts_step, 1)
            nc.gpsimd.memset(neg_half[:], -0.5).then_inc(consts_step, 1)
            nc.gpsimd.memset(eps[:], LN_EPS).then_inc(consts_step, 1)
            for a in range(2):
                nc.gpsimd.memset(v_t[a][:, 0:1], 0.0).then_inc(consts_step, 1)
                nc.gpsimd.memset(v_t[a][:, S + 1:S + 2], 0.0).then_inc(consts_step, 1)
            pool.wait_ge(consts_step, 7)
            nc.gpsimd.affine_select(out=ident[:], in_=zeros[:, 0:P], compare_op=ALU.not_equal, fill=1.0, base=0,
                                    pattern=[[-1, P]], channel_multiplier=1).then_inc(consts_ready, 1)
            nc.gpsimd.affine_select(out=mask[:].rearrange("p m j -> p (m j)"), in_=zeros[:], compare_op=ALU.is_ge, fill=MASKED,
                                    base=P, pattern=[[-1, 2 * P]], channel_multiplier=1).then_inc(consts_ready, 1)

            def rstd(job):
                k, n, _ = job
                pool.wait_ge(mv_done[k], T * (n + 1))
                nc.gpsimd.tensor_tensor(ln_var[k][:], ln_mv[k][:, :, 1], eps[:], ALU.add).then_inc(var_done[k], 1)
                pool.wait_ge(var_done[k], n + 1)
                nc.gpsimd.tensor_tensor(ln_rstd[k][:], ln_var[k][:], neg_half[:], ALU.pow).then_inc(rstd_done[k], 1)

            def conv_values(job):
                a, n = job[0] - ATTN, job[1]
                pool.wait_ge(v_ready[a], n + 1)
                for shift, (dst, tap) in enumerate(((prev_t, tap_prev), (mid_t, tap_mid), (next_t, neg_tap_next[:]))):
                    nc.gpsimd.tensor_tensor(dst[a][:], v_t[a][:, shift:shift + S], tap.to_broadcast([P, S]),
                                            ALU.mult).then_inc(taps_done[a], 1)
                pool.wait_ge(taps_done[a], 3 * (n + 1))
                nc.gpsimd.tensor_tensor(pm_t[a][:], prev_t[a][:], mid_t[a][:], ALU.add).then_inc(pm_done[a], 1)
                pool.wait_ge(pm_done[a], n + 1)
                nc.gpsimd.tensor_tensor(conv_t[a][:], pm_t[a][:], next_t[a][:], ALU.subtract).then_inc(conv_ready[a], 1)

            def add_diagonal(job):
                a, n, b = job[0] - ATTN, job[1], job[2]
                pool.wait_ge(conv_next_ready[a], n + 1)
                pool.wait_ge(diag_weight_ready[a], n + 1)
                nc.gpsimd.tensor_tensor(diag_term[a][:], conv_next[a][:, T:2 * T],
                                        diag_weight[a][:].unsqueeze(2).to_broadcast([P, T, D]), ALU.mult).then_inc(diag_term_done[a], 1)
                pool.wait_ge(diag_term_done[a], n + 1)
                nc.gpsimd.tensor_tensor(x_sb[:, b], x_sb[:, b], diag_term[a][:], ALU.add).then_inc(diag_added[a], 1)

            def make_w1_block(j):
                pool.wait_ge(scal_ready, 1)
                pool.wait_ge(k1_loaded, 16)
                nc.gpsimd.tensor_scalar(w1[:, j], k1_u8[:, j], w1_mul[:], w1_add[:], ALU.mult, ALU.add).then_inc(w1_ready, 1)

            def scale_cols():
                pool.wait_ge(cols_loaded, 16)
                nc.gpsimd.tensor_scalar(neg_tap_next[:], tap_next, -1.0, 1.0, ALU.mult, ALU.mult).then_inc(consts_step, 1)
                nc.gpsimd.tensor_scalar(scaled_bias_q[:], bias_q, ATTN_SCALE, 1.0, ALU.mult, ALU.mult).then_inc(consts_step, 1)

            rstd(ffn1(0))
            rstd(ffn1(1))
            make_w1_block(3)
            make_w1_block(2)
            rstd(ffn1(2))
            rstd(attn(0))
            scale_cols()
            pool.wait_ge(consts_step, 9)

            def iteration(t, first=False):
                one, att = ffn1(t), attn(t - 2)
                if not first:
                    rstd(ffn2(t - 4))
                rstd(one)
                conv_values(attn(t - 3))
                rstd(att)
                add_diagonal(attn(t - 3))

            iteration(LOOP_FROM - 1, first=True)
            with pool.Fori(LOOP_FROM, LOOP_TO - 1) as t:
                iteration(t)
            iteration(LOOP_TO - 1)

            rstd(ffn2(B - 4))
            conv_values(attn(B - 3))
            rstd(attn(B - 2))
            add_diagonal(attn(B - 3))
            rstd(attn(B - 1))
            rstd(ffn2(B - 3))
            conv_values(attn(B - 2))
            conv_values(attn(B - 1))
            add_diagonal(attn(B - 2))
            rstd(ffn2(B - 2))
            add_diagonal(attn(B - 1))
            rstd(ffn2(B - 1))

        @block.scalar
        def _(act):
            nc.scalar.preload_act_table(ACT.Exp)

            def split_hi_xt(job):
                s, n, _ = job
                act.wait_ge(xt_done[s], n + 1)
                nc.scalar.activation(xt_hi[s][:], ps_ffn[s][:, 0, 0:S], ACT.Copy, scale=XN_SCALE).then_inc(xt_hi_ready[s], 1)

            def split_hi(job, half, done, hi, ready):
                s, n, _ = job
                act.wait_ge(done[s], 2 * n + half + 1)
                nc.scalar.activation(hi[s][:, HALF * half:HALF * half + HALF], ps_ffn[s][:, half], ACT.Relu).then_inc(ready[s], 1)

            def h1_hi_half(job, half):
                split_hi(job, half, l1_done, h1_hi, h1_hi_ready)

            def h2_hi_half(job, half):
                split_hi(job, half, l2_done, h2_hi, h2_hi_ready)

            def copy_xt(job):
                a, n = job[0] - ATTN, job[1]
                act.wait_ge(xt_done[ATTN + a], n + 1)
                nc.scalar.copy(xt_attn[a][:], ps_attn[a][:, 1, 0:S]).then_inc(xt_attn_ready[a], 1)

            def kv_bias(job):
                a, n = job[0] - ATTN, job[1]
                act.wait_ge(kv_done[a], n + 1)
                nc.scalar.activation(k_t[a][:], ps_attn[a][:, 1, 0:S], ACT.Identity, bias=bias_k).then_inc(k_ready[a], 1)
                if after_first(n):
                    act.wait_ge(conv_ready[a], n)
                nc.scalar.activation(v_t[a][:, 1:S + 1], ps_attn[a][:, 1, S:2 * S], ACT.Identity, bias=bias_v).then_inc(v_ready[a], 1)

            def q_bias_scale(job):
                a, n = job[0] - ATTN, job[1]
                act.wait_ge(q_done[a], n + 1)
                nc.scalar.activation(q_t[a][:], ps_attn[a][:, 0, 0:S], ACT.Identity, bias=scaled_bias_q[:],
                                     scale=ATTN_SCALE).then_inc(q_ready[a], 1)

            def softmax_exp(job):
                a, n = job[0] - ATTN, job[1]
                for i, blocks in enumerate((slice(0, 1), slice(1, 3))):
                    act.wait_ge(max_ready[a], T * n + i + 1)
                    nc.scalar.activation(prob[a][:, blocks], neg_scores[a][:, blocks], ACT.Exp, bias=neg_max[a][:, i:i + 1],
                                         scale=-1.0, accum_out=prob_sum[a][:, i:i + 1]).then_inc(probs_ready[a], 1)

            def copy_conv_next(job):
                a, n = job[0] - ATTN, job[1]
                act.wait_ge(conv_next_done[a], n + 1)
                nc.scalar.copy(conv_next[a][:], ps_attn[a][:, 0]).then_inc(conv_next_ready[a], 1)

            def copy_prob_t(job):
                a, n = job[0] - ATTN, job[1]
                act.wait_ge(prob_t_done[a], n + 1)
                nc.scalar.copy(prob_t[a][:], ps_attn[a][:, 1, 0:3 * P]).then_inc(prob_t_ready[a], 1)

            def make_w1():
                act.wait_ge(scal_ready, 1)
                act.wait_ge(k1_loaded, 16)
                nc.scalar.activation(w1[:, 0:HALF], k1_u8[:, 0:HALF], ACT.Identity, bias=w1_add[:],
                                     scale=w1_mul[:]).then_inc(w1_ready, 1)

            make_w1()
            split_hi_xt(ffn1(0))
            split_hi_xt(ffn1(1))
            h1_hi_half(ffn1(0), 0)
            h1_hi_half(ffn1(0), 1)
            h1_hi_half(ffn1(1), 0)
            h1_hi_half(ffn1(1), 1)
            h2_hi_half(ffn1(0), 0)
            h2_hi_half(ffn1(0), 1)
            split_hi_xt(ffn1(2))
            h2_hi_half(ffn1(1), 0)
            h2_hi_half(ffn1(1), 1)
            h1_hi_half(ffn1(2), 0)
            h1_hi_half(ffn1(2), 1)
            act.wait_ge(cols_loaded, 16)
            act.wait_ge(consts_step, 9)
            copy_xt(attn(0))
            kv_bias(attn(0))
            q_bias_scale(attn(0))
            h2_hi_half(ffn1(2), 0)
            softmax_exp(attn(0))
            h2_hi_half(ffn1(2), 1)
            split_hi_xt(ffn1(3))
            copy_conv_next(attn(0))
            copy_prob_t(attn(0))
            copy_xt(attn(1))

            def iteration(t, first=False, last=False):
                one, att, two = ffn1(t), attn(t - 2), ffn2(t - 3)
                h1_hi_half(one, 0)
                h1_hi_half(one, 1)
                kv_bias(att)
                if not first:
                    h2_hi_half(ffn2(t - 4), 1)
                q_bias_scale(att)
                split_hi_xt(two)
                h2_hi_half(one, 0)
                softmax_exp(att)
                h2_hi_half(one, 1)
                h1_hi_half(two, 0)
                if not last:
                    split_hi_xt(ffn1(t + 1))
                copy_prob_t(att)
                h1_hi_half(two, 1)
                copy_conv_next(att)
                copy_xt(attn(t - 1))
                h2_hi_half(two, 0)

            iteration(LOOP_FROM - 1, first=True)
            with act.Fori(LOOP_FROM, LOOP_TO - 1) as t:
                iteration(t)
            iteration(LOOP_TO - 1, last=True)

            kv_bias(attn(B - 2))
            q_bias_scale(attn(B - 2))
            copy_xt(attn(B - 1))
            h2_hi_half(ffn2(B - 4), 1)
            kv_bias(attn(B - 1))
            q_bias_scale(attn(B - 1))
            split_hi_xt(ffn2(B - 3))
            softmax_exp(attn(B - 2))
            copy_conv_next(attn(B - 2))
            h1_hi_half(ffn2(B - 3), 0)
            copy_prob_t(attn(B - 2))
            h1_hi_half(ffn2(B - 3), 1)
            softmax_exp(attn(B - 1))
            h2_hi_half(ffn2(B - 3), 0)
            copy_conv_next(attn(B - 1))
            copy_prob_t(attn(B - 1))
            split_hi_xt(ffn2(B - 2))
            h2_hi_half(ffn2(B - 3), 1)
            h1_hi_half(ffn2(B - 2), 0)
            h1_hi_half(ffn2(B - 2), 1)
            split_hi_xt(ffn2(B - 1))
            h1_hi_half(ffn2(B - 1), 0)
            h1_hi_half(ffn2(B - 1), 1)
            h2_hi_half(ffn2(B - 2), 0)
            h2_hi_half(ffn2(B - 1), 0)
            h2_hi_half(ffn2(B - 2), 1)
            h2_hi_half(ffn2(B - 1), 1)

        @block.vector
        def _(dve):
            def wait_apart(semaphore, value):
                if not isinstance(value, int):
                    dve.to_reg(value)
                    dve.wait_ge(scalars_loaded, 16)
                dve.wait_ge(semaphore, value)

            def ln_moments(job, source):
                k, n, b = job
                if source is None:
                    part = next(i for i, (_, z) in enumerate(X_PARTS) if b < z) if isinstance(b, int) else len(X_PARTS) - 1
                    dve.wait_ge(x_loaded[part], 16)
                else:
                    wait_apart(added[source[0]], source[1] + 1)
                for i in range(T):
                    nc.vector.bn_stats(ln_stats[k][:, i], x_sb[:, b, i]).then_inc(stats_done[k], 1)
                wait_apart(stats_done[k], T * (n + 1))
                for i in range(T):
                    nc.vector.bn_aggr(ln_mv[k][:, i], ln_stats[k][:, i]).then_inc(mv_done[k], 1)

            def ln_apply(job):
                k, n, b = job
                dve.wait_ge(rstd_done[k], n + 1)
                if after_first(n):
                    dve.wait_ge(xt_done[k], n)
                for i in range(T):
                    nc.vector.tensor_scalar(xn[k][:, i], x_sb[:, b, i], ln_mv[k][:, i, 0:1],
                                            ln_rstd[k][:, i:i + 1], ALU.subtract, ALU.mult).then_inc(xn_ready[k], 1)

            def split_lo_xt(job):
                s, n, _ = job
                dve.wait_ge(xt_hi_ready[s], n + 1)
                nc.vector.scalar_tensor_tensor(out=xt_lo[s][:], in0=ps_ffn[s][:, 0, 0:S], scalar=XN_SCALE, in1=xt_hi[s][:],
                                               op0=ALU.mult, op1=ALU.subtract).then_inc(xt_lo_ready[s], 1)

            def split_lo(job, half, hi, lo, hi_ready, lo_ready):
                s, n, _ = job
                dve.wait_ge(hi_ready[s], 2 * n + half + 1)
                blocks = slice(HALF * half, HALF * half + HALF)
                nc.vector.scalar_tensor_tensor(out=lo[s][:, blocks], in0=ps_ffn[s][:, half], scalar=0.0, in1=hi[s][:, blocks],
                                               op0=ALU.max, op1=ALU.subtract).then_inc(lo_ready[s], 1)

            def h1_lo_half(job, half):
                split_lo(job, half, h1_hi, h1_lo, h1_hi_ready, h1_lo_ready)

            def h2_lo_half(job, half):
                split_lo(job, half, h2_hi, h2_lo, h2_hi_ready, h2_lo_ready)

            def ffn_residual(job):
                s, n, b = job
                dve.wait_ge(l3_done[s], n + 1)
                nc.vector.scalar_tensor_tensor(out=x_sb[:, b], in0=ps_ffn[s][:, 1, 0:T * D], scalar=ffn_fac[:], in1=x_sb[:, b],
                                               op0=ALU.mult, op1=ALU.add).then_inc(added[s], 1)

            def softmax_max(job):
                a, n = job[0] - ATTN, job[1]
                wait_apart(scores_done[a], n + 1)
                for i, (lo, hi) in enumerate(((0, 1), (1, 3))):
                    nc.vector.tensor_tensor_reduce(neg_scores[a][:, lo:hi], ps_attn[a][:, 1, lo * P:hi * P].rearrange("p (m j) -> p m j", j=P),
                                                   mask[:, 1 - i:2], -1.0, -MASKED, ALU.add, ALU.min,
                                                   neg_max[a][:, i:i + 1]).then_inc(max_ready[a], 1)

            def softmax_weights(job):
                a, n = job[0] - ATTN, job[1]
                dve.wait_ge(probs_ready[a], T * (n + 1))
                nc.vector.reciprocal(prob_inv[a][:], prob_sum[a][:]).then_inc(inv_ready[a], 1)
                for i in range(T):
                    nc.vector.tensor_tensor_reduce(diag_block[a][:, i], prob[a][:, 2 * i], ident[:], 1.0, 0.0, ALU.mult, ALU.add,
                                                   prob_diag[a][:, i:i + 1]).then_inc(diag_done[a], 1)
                dve.wait_ge(inv_ready[a], n + 1)
                dve.wait_ge(diag_done[a], T * (n + 1))
                nc.vector.tensor_tensor(diag_weight[a][:], prob_diag[a][:], prob_inv[a][:], ALU.mult).then_inc(diag_weight_ready[a], 1)

            def attn_residual(job):
                a, n, b = job[0] - ATTN, job[1], job[2]
                dve.wait_ge(diag_added[a], n + 1)
                dve.wait_ge(attn_out_done[a], n + 1)
                for i in range(T):
                    last = nc.vector.scalar_tensor_tensor(out=x_sb[:, b, i], in0=ps_attn[a][:, 0, i * D:(i + 1) * D],
                                                          scalar=prob_inv[a][:, i:i + 1], in1=x_sb[:, b, i],
                                                          op0=ALU.mult, op1=ALU.add)
                last.then_inc(added[ATTN + a], 1)

            def sign_weights():
                dve.wait_ge(scalars_loaded, 16)
                nc.vector.tensor_scalar(s_pos[:], s_cols[:, 0:2], 0.0, None, ALU.is_gt).then_inc(scal_step, 1)
                nc.vector.tensor_scalar(s_neg[:], s_cols[:, 0:2], 0.0, None, ALU.is_lt).then_inc(scal_step, 1)
                dve.wait_ge(scal_step, 2)
                nc.vector.tensor_tensor(s_sign[:], s_pos[:], s_neg[:], ALU.subtract).then_inc(scal_step, 1)
                dve.wait_ge(scal_step, 3)
                nc.vector.tensor_scalar(w1_mul[:], s_sign[:, 1:2], 2.0 * W1_SCALE, None, ALU.mult)
                nc.vector.tensor_scalar(w1_add[:], s_sign[:, 1:2], -W1_SCALE, None, ALU.mult).then_inc(scal_ready, 1)

            def diff_w0():
                dve.wait_ge(k0_loaded, 16)
                nc.vector.tensor_tensor(w0_diff[:], k0_u8[:, 0], k0_u8[:, 1], ALU.subtract).then_inc(w0_step, 1)

            def sign_w0():
                dve.wait_ge(w0_step, 1)
                nc.vector.tensor_scalar(w0[:], w0_diff[:], s_sign[:, 0:1], None, ALU.mult).then_inc(w0_ready, 1)

            def size_factors():
                nc.vector.tensor_tensor(s_abs[:], s_cols[:, 0:2], s_sign[:], ALU.mult).then_inc(scal_step, 1)

            def size_product():
                dve.wait_ge(scal_step, 4)
                nc.vector.tensor_tensor(ffn_fac_a[:], s_abs[:, 0:1], s_abs[:, 1:2], ALU.mult).then_inc(scal_step, 1)

            def result_factor():
                dve.wait_ge(scal_step, 5)
                nc.vector.scalar_tensor_tensor(out=ffn_fac[:], in0=ffn_fac_a[:], scalar=FINAL_SCALE, in1=s_cols[:, 2:3],
                                               op0=ALU.mult, op1=ALU.mult).then_inc(fac_ready, 1)

            def make_w2():
                dve.wait_ge(k2_loaded, 16)
                nc.vector.tensor_scalar(w2[:], k2_u8[:], 2.0, -1.0, ALU.mult, ALU.add).then_inc(w2_ready, 1)

            nc.vector.memset(warm[:], 0.0).then_inc(warm_ready, 1)
            ln_moments(ffn1(0), None)
            ln_moments(ffn1(1), None)
            sign_weights()
            ln_apply(ffn1(0))
            diff_w0()
            ln_apply(ffn1(1))
            sign_w0()
            split_lo_xt(ffn1(0))
            split_lo_xt(ffn1(1))
            size_factors()
            size_product()
            h1_lo_half(ffn1(0), 0)
            h1_lo_half(ffn1(0), 1)
            ln_moments(ffn1(2), None)
            result_factor()
            make_w2()
            h1_lo_half(ffn1(1), 0)
            ln_apply(ffn1(2))
            h1_lo_half(ffn1(1), 1)
            h2_lo_half(ffn1(0), 0)
            h2_lo_half(ffn1(0), 1)
            dve.wait_ge(fac_ready, 1)
            ffn_residual(ffn1(0))
            ln_moments(attn(0), ffn1(0))
            h2_lo_half(ffn1(1), 0)
            split_lo_xt(ffn1(2))
            ln_apply(attn(0))
            h2_lo_half(ffn1(1), 1)
            h1_lo_half(ffn1(2), 0)
            ln_moments(ffn1(3), None)
            ffn_residual(ffn1(1))
            h1_lo_half(ffn1(2), 1)
            ln_moments(attn(1), ffn1(1))
            ln_apply(ffn1(3))
            dve.wait_ge(consts_ready, 2)
            softmax_max(attn(0))
            h2_lo_half(ffn1(2), 0)
            softmax_weights(attn(0))
            h2_lo_half(ffn1(2), 1)

            def iteration(t, first=False, last=False):
                one, att, two = ffn1(t), attn(t - 2), ffn2(t - 3)
                if not first:
                    h1_lo_half(ffn2(t - 4), 0)
                split_lo_xt(one)
                ln_apply(att)
                if not first:
                    h1_lo_half(ffn2(t - 4), 1)
                if not last:
                    ln_moments(ffn1(t + 1), None)
                ffn_residual(ffn1(t - 1))
                attn_residual(attn(t - 3))
                if not first:
                    h2_lo_half(ffn2(t - 4), 0)
                ln_moments(two, attn(t - 3))
                h1_lo_half(one, 0)
                h1_lo_half(one, 1)
                if not first:
                    h2_lo_half(ffn2(t - 4), 1)
                ln_apply(two)
                ln_moments(attn(t - 1), ffn1(t - 1))
                if not last:
                    ln_apply(ffn1(t + 1))
                softmax_max(att)
                split_lo_xt(two)
                h2_lo_half(one, 0)
                softmax_weights(att)
                if not first:
                    ffn_residual(ffn2(t - 4))
                h2_lo_half(one, 1)

            iteration(LOOP_FROM - 1, first=True)
            with dve.Fori(LOOP_FROM, LOOP_TO - 1) as t:
                iteration(t)
            iteration(LOOP_TO - 1, last=True)

            h1_lo_half(ffn2(B - 4), 0)
            ln_apply(attn(B - 2))
            h1_lo_half(ffn2(B - 4), 1)
            ffn_residual(ffn1(B - 1))
            ln_moments(attn(B - 1), ffn1(B - 1))
            attn_residual(attn(B - 3))
            ln_moments(ffn2(B - 3), attn(B - 3))
            ln_apply(attn(B - 1))
            ln_apply(ffn2(B - 3))
            h2_lo_half(ffn2(B - 4), 0)
            h2_lo_half(ffn2(B - 4), 1)
            softmax_max(attn(B - 2))
            split_lo_xt(ffn2(B - 3))
            ffn_residual(ffn2(B - 4))
            softmax_weights(attn(B - 2))
            h1_lo_half(ffn2(B - 3), 0)
            h1_lo_half(ffn2(B - 3), 1)
            softmax_max(attn(B - 1))
            attn_residual(attn(B - 2))
            ln_moments(ffn2(B - 2), attn(B - 2))
            softmax_weights(attn(B - 1))
            ln_apply(ffn2(B - 2))
            h2_lo_half(ffn2(B - 3), 0)
            split_lo_xt(ffn2(B - 2))
            attn_residual(attn(B - 1))
            ln_moments(ffn2(B - 1), attn(B - 1))
            h2_lo_half(ffn2(B - 3), 1)
            h1_lo_half(ffn2(B - 2), 0)
            ln_apply(ffn2(B - 1))
            h1_lo_half(ffn2(B - 2), 1)
            ffn_residual(ffn2(B - 3))
            split_lo_xt(ffn2(B - 1))
            h1_lo_half(ffn2(B - 1), 0)
            h1_lo_half(ffn2(B - 1), 1)
            h2_lo_half(ffn2(B - 2), 0)
            h2_lo_half(ffn2(B - 1), 0)
            h2_lo_half(ffn2(B - 2), 1)
            h2_lo_half(ffn2(B - 1), 1)
            ffn_residual(ffn2(B - 2))
            ffn_residual(ffn2(B - 1))

        @block.tensor
        def _(pe):
            def transpose_rows(job):
                k, n, _ = job
                ps, bank = (ps_attn[k - ATTN], 1) if k >= ATTN else (ps_ffn[k], 0)
                if after_first(n):
                    if k >= ATTN:
                        pe.wait_ge(prob_t_ready[k - ATTN], n)
                    else:
                        pe.wait_ge(h2_lo_ready[k], 2 * n - 1)
                for i in range(T):
                    pe.wait_ge(xn_ready[k], T * n + i + 1)
                    last = nc.tensor.transpose(ps[:, bank, i * P:(i + 1) * P], xn[k][:, i], ident[:])
                last.then_inc(xt_done[k], 1)

            def layer1_half(job, half):
                s, n, _ = job
                if half == 0:
                    pe.wait_ge(xt_lo_ready[s], n + 1)
                elif after_first(n):
                    pe.wait_ge(added[s], n)
                for c in range(HALF):
                    block_out = HALF * half + c
                    w = w0[:, block_out * P:(block_out + 1) * P]
                    dst = ps_ffn[s][:, half, c * S:(c + 1) * S]
                    nc.tensor.matmul(dst, w, xt_hi[s][:], start=True, stop=False)
                    last = nc.tensor.matmul(dst, w, xt_lo[s][:], start=False, stop=True)
                last.then_inc(l1_done[s], 1)

            def layer2_half(job, half):
                s, n, _ = job
                for c in range(HALF):
                    block_out = HALF * half + c
                    dst = ps_ffn[s][:, half, c * S:(c + 1) * S]
                    for j in range(FB):
                        if half == 0 and c == 0 and j % HALF == 0:
                            pe.wait_ge(h1_lo_ready[s], 2 * n + j // HALF + 1)
                        w = w1[:, j, block_out * P:(block_out + 1) * P]
                        nc.tensor.matmul(dst, w, h1_hi[s][:, j], start=(j == 0), stop=False)
                        last = nc.tensor.matmul(dst, w, h1_lo[s][:, j], start=False, stop=(j == FB - 1))
                last.then_inc(l2_done[s], 1)

            def layer3(job):
                s, n, _ = job
                pe.wait_ge(h2_lo_ready[s], 2 * (n + 1))
                for i in range(T):
                    for j in range(FB):
                        rows = slice(i * P, (i + 1) * P)
                        dst = ps_ffn[s][:, 1, i * D:(i + 1) * D]
                        nc.tensor.matmul(dst, h2_hi[s][:, j, rows], w2[:, j], start=(j == 0), stop=False)
                        last = nc.tensor.matmul(dst, h2_lo[s][:, j, rows], w2[:, j], start=False, stop=(j == FB - 1))
                last.then_inc(l3_done[s], 1)

            def project_kv(job):
                a, n = job[0] - ATTN, job[1]
                pe.wait_ge(xt_attn_ready[a], n + 1)
                nc.tensor.matmul(ps_attn[a][:, 1, 0:S], wqkv[:, 1], xt_attn[a][:], start=True, stop=True)
                nc.tensor.matmul(ps_attn[a][:, 1, S:2 * S], wqkv[:, 2], xt_attn[a][:], start=True, stop=True).then_inc(kv_done[a], 1)

            def project_q(job):
                a, n = job[0] - ATTN, job[1]
                if after_first(n):
                    pe.wait_ge(added[ATTN + a], n)
                nc.tensor.matmul(ps_attn[a][:, 0, 0:S], wqkv[:, 0], xt_attn[a][:], start=True, stop=True).then_inc(q_done[a], 1)

            def scores(job):
                a, n = job[0] - ATTN, job[1]
                ps = ps_attn[a]
                pe.wait_ge(q_ready[a], n + 1)
                pe.wait_ge(k_ready[a], n + 1)
                pe.wait_ge(v_ready[a], n + 1)
                nc.tensor.matmul(ps[:, 1, 0:P], q_t[a][:, 0:P], k_t[a][:, 0:P], start=True, stop=True)
                nc.tensor.matmul(ps[:, 1, P:3 * P], q_t[a][:, P:S], k_t[a][:], start=True, stop=True).then_inc(scores_done[a], 1)

            def transpose_conv(job):
                a, n = job[0] - ATTN, job[1]
                pe.wait_ge(conv_ready[a], n + 1)
                for m, src in enumerate((conv_t, next_t)):
                    for i in range(T):
                        last = nc.tensor.transpose(ps_attn[a][:, 0, (T * m + i) * P:(T * m + i + 1) * P],
                                                   src[a][:, i * P:(i + 1) * P], ident[:])
                last.then_inc(conv_next_done[a], 1)

            def transpose_probs(job):
                a, n = job[0] - ATTN, job[1]
                pe.wait_ge(probs_ready[a], T * (n + 1))
                for m in range(3):
                    last = nc.tensor.transpose(ps_attn[a][:, 1, m * P:(m + 1) * P], prob[a][:, m], ident[:])
                last.then_inc(prob_t_done[a], 1)

            def attend(job):
                a, n = job[0] - ATTN, job[1]
                pe.wait_ge(conv_next_ready[a], n + 1)
                pe.wait_ge(prob_t_ready[a], n + 1)
                for i in range(T):
                    for j in range(i + 1):
                        last = nc.tensor.matmul(ps_attn[a][:, 0, i * D:(i + 1) * D], prob_t[a][:, i + j], conv_next[a][:, j],
                                                start=(j == 0), stop=(j == i))
                last.then_inc(attn_out_done[a], 1)

            def warm_up(count):
                for _ in range(count):
                    nc.tensor.matmul(ps_attn[1][:, 0], warm[:, 0:P], warm[:], start=True, stop=True)

            pe.wait_ge(warm_ready, 1)
            warm_up(WARM_UP)
            pe.wait_ge(consts_ready, 2)
            transpose_rows(ffn1(0))
            transpose_rows(ffn1(1))
            pe.wait_ge(w0_ready, 1)
            layer1_half(ffn1(0), 0)
            layer1_half(ffn1(0), 1)
            warm_up(WARM_UP_MORE)
            layer1_half(ffn1(1), 0)
            layer1_half(ffn1(1), 1)
            pe.wait_ge(w1_ready, 1 + HALF)
            layer2_half(ffn1(0), 0)
            layer2_half(ffn1(0), 1)
            layer2_half(ffn1(1), 0)
            pe.wait_ge(w2_ready, 1)
            layer3(ffn1(0))
            transpose_rows(ffn1(2))
            layer2_half(ffn1(1), 1)
            layer1_half(ffn1(2), 0)
            layer1_half(ffn1(2), 1)
            transpose_rows(attn(0))
            layer3(ffn1(1))
            pe.wait_ge(wqkv_loaded, 16)
            project_kv(attn(0))
            project_q(attn(0))
            layer2_half(ffn1(2), 0)
            scores(attn(0))
            layer2_half(ffn1(2), 1)
            transpose_rows(ffn1(3))
            transpose_probs(attn(0))
            transpose_conv(attn(0))
            layer3(ffn1(2))
            attend(attn(0))
            transpose_rows(attn(1))
            layer1_half(ffn1(3), 0)
            layer1_half(ffn1(3), 1)

            def iteration(t, first=False, last=False):
                one, att, two = ffn1(t), attn(t - 2), ffn2(t - 3)
                project_kv(att)
                if not first:
                    layer2_half(ffn2(t - 4), 1)
                project_q(att)
                layer2_half(one, 0)
                transpose_rows(two)
                scores(att)
                layer2_half(one, 1)
                if not first:
                    layer3(ffn2(t - 4))
                layer1_half(two, 0)
                transpose_probs(att)
                if not last:
                    transpose_rows(ffn1(t + 1))
                layer1_half(two, 1)
                transpose_conv(att)
                layer3(one)
                if not last:
                    layer1_half(ffn1(t + 1), 0)
                transpose_rows(attn(t - 1))
                attend(att)
                layer2_half(two, 0)
                if not last:
                    layer1_half(ffn1(t + 1), 1)

            iteration(LOOP_FROM - 1, first=True)
            with pe.Fori(LOOP_FROM, LOOP_TO - 1) as t:
                iteration(t)
            iteration(LOOP_TO - 1, last=True)

            project_kv(attn(B - 2))
            project_q(attn(B - 2))
            transpose_rows(attn(B - 1))
            layer2_half(ffn2(B - 4), 1)
            project_kv(attn(B - 1))
            project_q(attn(B - 1))
            scores(attn(B - 2))
            transpose_rows(ffn2(B - 3))
            layer3(ffn2(B - 4))
            transpose_conv(attn(B - 2))
            layer1_half(ffn2(B - 3), 0)
            transpose_probs(attn(B - 2))
            layer1_half(ffn2(B - 3), 1)
            scores(attn(B - 1))
            attend(attn(B - 2))
            transpose_conv(attn(B - 1))
            layer2_half(ffn2(B - 3), 0)
            transpose_probs(attn(B - 1))
            layer2_half(ffn2(B - 3), 1)
            transpose_rows(ffn2(B - 2))
            attend(attn(B - 1))
            layer1_half(ffn2(B - 2), 0)
            layer1_half(ffn2(B - 2), 1)
            layer3(ffn2(B - 3))
            transpose_rows(ffn2(B - 1))
            layer2_half(ffn2(B - 2), 0)
            layer1_half(ffn2(B - 1), 0)
            layer1_half(ffn2(B - 1), 1)
            layer2_half(ffn2(B - 2), 1)
            layer2_half(ffn2(B - 1), 0)
            layer2_half(ffn2(B - 1), 1)
            layer3(ffn2(B - 2))
            layer3(ffn2(B - 1))


def kernel(**inputs):
    import numpy as np
    import concourse.bacc as bacc
    from concourse.bass_utils import run_bass_kernel_spmd

    a = {name.split("_", 2)[2]: np.ascontiguousarray(v) for name, v in inputs.items()}
    arrays = {
        "x": a["x"],
        "w_qkv": a["W_qkv"],
        "attn_cols": np.concatenate([a["b_qkv"].reshape(3, -1).T, a["W_vconv"]], axis=1),
        "k0": a["k0"],
        "k1": a["k1"],
        "k2": a["k2"],
        "scalars": np.concatenate([a[s].reshape(1, 1) for s in ("s0", "s1", "s2")], axis=1),
    }
    nc = bacc.Bacc("TRN2", target_bir_lowering=False, num_devices=1)
    args = [nc.dram_tensor(f"in_{name}", v.shape, mybir.dt.from_np(v.dtype), kind="ExternalInput").ap()
            for name, v in arrays.items()]
    out = nc.dram_tensor("out_y", a["x"].shape, F32, kind="ExternalOutput").ap()
    macaron_kernel(nc, *args, out)
    r = run_bass_kernel_spmd(nc, [{f"in_{name}": np.ascontiguousarray(v) for name, v in arrays.items()}], core_ids=[0])
    return r.results[0]["out_y"]
```
